# Optimizing a Trainium2 kernel written in Bass

```python
import numpy as np
import jax
import jax.numpy as jnp

def _softmax(x, axis=-1):
    return jax.nn.softmax(x, axis=axis)

def _gelu(x):
    return jax.nn.gelu(x, approximate=True)

def _silu(x):
    return jax.nn.silu(x)

def _sigmoid(x):
    return jax.nn.sigmoid(x)

def _layernorm(x, axis=-1, eps=1e-05):
    m = jnp.mean(x, axis=axis, keepdims=True)
    v = jnp.var(x, axis=axis, keepdims=True)
    return (x - m) / jnp.sqrt(v + eps)

def _scatter_add(tgt, idx, src, axis=0):
    return tgt.at[idx].add(src)

def _segment_sum(src, seg, n):
    return jax.ops.segment_sum(src, seg, n)
kernel_name = 'mk_prb_d4_jaxref_r8_4963f0'

def setup_inputs(seed: int=0):
    np.random.seed(seed)
    _w = jnp.asarray

    def _L0_attn_setup():
        import jax, jax.numpy as jnp
        import numpy as np
        D_MODEL = 128
        D_INNER = 256
        D_STATE = 16
        DT_RANK = 64
        K_CONV = 4
        D_FF = 512
        EPS = 1e-06

        def _rms(x, w):
            return x * jax.lax.rsqrt(jnp.mean(x * x, axis=-1, keepdims=True) + EPS) * w

        def _reference_tuple_inner(hidden_states, in_proj_w, conv_w, conv_b, x_proj_w, dt_proj_w, dt_proj_b, dt_ln_w, b_ln_w, c_ln_w, A_log, D_skip, out_proj_w, input_ln_w, pre_moe_ln_w, gate_w, up_w, down_w):
            B, S, _ = hidden_states.shape
            residual = hidden_states
            h = _rms(hidden_states, input_ln_w)
            xz = h @ in_proj_w
            x, z = jnp.split(xz, 2, axis=-1)
            xt = jnp.transpose(x, (0, 2, 1))
            conv_state = xt[:, :, -K_CONV:]
            y = jax.lax.conv_general_dilated(xt, conv_w[:, None, :], window_strides=(1,), padding=[(K_CONV - 1, 0)], feature_group_count=D_INNER, dimension_numbers=('NCH', 'OIH', 'NCH'))
            y = y + conv_b[None, :, None]
            x = jax.nn.silu(jnp.transpose(y, (0, 2, 1)))
            proj = x @ x_proj_w
            dt_raw = proj[..., :DT_RANK]
            B_raw = proj[..., DT_RANK:DT_RANK + D_STATE]
            C_raw = proj[..., DT_RANK + D_STATE:]
            dt = jax.nn.softplus(_rms(dt_raw, dt_ln_w) @ dt_proj_w + dt_proj_b)
            Bm = _rms(B_raw, b_ln_w)
            Cm = _rms(C_raw, c_ln_w)
            A = -jnp.exp(A_log)

            def step(hstate, ins):
                x_t, dt_t, B_t, C_t = ins
                dA = jnp.exp(dt_t[..., None] * A)
                hstate = hstate * dA + (dt_t * x_t)[..., None] * B_t[:, None, :]
                y_t = jnp.einsum('bdn,bn->bd', hstate, C_t)
                return (hstate, y_t)
            h0 = jnp.zeros((B, D_INNER, D_STATE), x.dtype)
            xs = (jnp.swapaxes(x, 0, 1), jnp.swapaxes(dt, 0, 1), jnp.swapaxes(Bm, 0, 1), jnp.swapaxes(Cm, 0, 1))
            ssm_state, ys = jax.lax.scan(step, h0, xs)
            y = jnp.swapaxes(ys, 0, 1) + x * D_skip
            y = y * jax.nn.silu(z)
            mamba_out = y @ out_proj_w
            hidden = residual + mamba_out
            residual = hidden
            hn = _rms(hidden, pre_moe_ln_w)
            ff = jax.nn.silu(hn @ gate_w) * (hn @ up_w) @ down_w
            out = residual + ff
            return (out, conv_state, ssm_state)
        key = jax.random.key(seed)
        ks = jax.random.split(key, 20)
        s = lambda i, shape, scale: jax.random.normal(ks[i], shape, dtype=jnp.float32) * scale
        inp = {'hidden_states': s(0, (2, 256, D_MODEL), 1.0), 'in_proj_w': s(1, (D_MODEL, 2 * D_INNER), D_MODEL ** (-0.5)), 'conv_w': s(2, (D_INNER, K_CONV), 0.3), 'conv_b': jnp.zeros((D_INNER,), jnp.float32), 'x_proj_w': s(3, (D_INNER, DT_RANK + 2 * D_STATE), D_INNER ** (-0.5)), 'dt_proj_w': s(4, (DT_RANK, D_INNER), DT_RANK ** (-0.5)), 'dt_proj_b': jnp.full((D_INNER,), -2.0, jnp.float32), 'dt_ln_w': jnp.ones((DT_RANK,), jnp.float32), 'b_ln_w': jnp.ones((D_STATE,), jnp.float32), 'c_ln_w': jnp.ones((D_STATE,), jnp.float32), 'A_log': jnp.log(jnp.broadcast_to(jnp.arange(1, D_STATE + 1, dtype=jnp.float32), (D_INNER, D_STATE))), 'D_skip': jnp.ones((D_INNER,), jnp.float32), 'out_proj_w': s(5, (D_INNER, D_MODEL), D_INNER ** (-0.5)), 'input_ln_w': jnp.ones((D_MODEL,), jnp.float32), 'pre_moe_ln_w': jnp.ones((D_MODEL,), jnp.float32), 'gate_w': s(6, (D_MODEL, D_FF), D_MODEL ** (-0.5)), 'up_w': s(7, (D_MODEL, D_FF), D_MODEL ** (-0.5)), 'down_w': s(8, (D_FF, D_MODEL), D_FF ** (-0.5))}
        return inp
    _L0_attn_in = _L0_attn_setup()

    def _L0_ffn_setup():
        import jax, jax.numpy as jnp
        import numpy as np
        B, S, D = (4, 128, 128)
        I = 64
        E = 32
        TOP_K = 8
        N_GROUP = 8
        TOPK_GROUP = 4

        def _group_topk(scores):
            T = scores.shape[0]
            epg = E // N_GROUP
            group_scores = scores.reshape(T, N_GROUP, epg).sum(axis=-1)
            _, top_groups = jax.lax.top_k(group_scores, TOPK_GROUP)
            group_mask = jnp.zeros((T, N_GROUP), scores.dtype).at[jnp.arange(T)[:, None], top_groups].set(1.0)
            expert_mask = jnp.repeat(group_mask, epg, axis=1)
            masked_scores = scores * expert_mask
            topk_w, topk_i = jax.lax.top_k(masked_scores, TOP_K)
            return (topk_w, topk_i)

        def _reference_tuple_inner(hidden_states, gate_w, expert_gate, expert_up, expert_down, shared_gate_w, shared_up_w, shared_down_w):
            b, s, d = hidden_states.shape
            flat = hidden_states.reshape(-1, d)
            T = flat.shape[0]
            logits = flat @ gate_w.T
            scores = jax.nn.sigmoid(logits)
            topk_w, topk_i = _group_topk(scores)
            topk_w = topk_w / jnp.clip(topk_w.sum(axis=-1, keepdims=True), 1e-12)
            combine = jnp.zeros((T, E), flat.dtype).at[jnp.arange(T)[:, None], topk_i].add(topk_w)

            def body(acc, expert):
                wg, wu, wd, w = expert
                h = jax.nn.silu(flat @ wg.T) * (flat @ wu.T)
                return (acc + w[:, None] * (h @ wd.T), None)
            out, _ = jax.lax.scan(body, jnp.zeros_like(flat), (expert_gate, expert_up, expert_down, combine.T))
            shared = jax.nn.silu(flat @ shared_gate_w.T) * (flat @ shared_up_w.T) @ shared_down_w.T
            out = out + shared
            return (out.reshape(b, s, d), logits)
        key = jax.random.key(seed)
        ks = jax.random.split(key, 8)
        scale = 0.02
        return {'hidden_states': jax.random.normal(ks[0], (B, S, D), jnp.float32), 'gate_w': jax.random.normal(ks[1], (E, D), jnp.float32) * scale, 'expert_gate': jax.random.normal(ks[2], (E, I, D), jnp.float32) * scale, 'expert_up': jax.random.normal(ks[3], (E, I, D), jnp.float32) * scale, 'expert_down': jax.random.normal(ks[4], (E, D, I), jnp.float32) * scale, 'shared_gate_w': jax.random.normal(ks[5], (I, D), jnp.float32) * scale, 'shared_up_w': jax.random.normal(ks[6], (I, D), jnp.float32) * scale, 'shared_down_w': jax.random.normal(ks[7], (D, I), jnp.float32) * scale}
    _L0_ffn_in = _L0_ffn_setup()

    def _L1_attn_setup():
        import jax, jax.numpy as jnp
        import numpy as np
        D = 128
        B = 4
        S = 512
        LN_EPS = 1e-05

        def _layer_norm(x, gamma, beta):
            mu = jnp.mean(x, axis=-1, keepdims=True)
            var = jnp.mean(jnp.square(x - mu), axis=-1, keepdims=True)
            return (x - mu) * jax.lax.rsqrt(var + LN_EPS) * gamma + beta
        key = jax.random.key(seed)
        ks = jax.random.split(key, 5)
        scale = 1.0 / np.sqrt(D)
        return {'hidden_states': jax.random.normal(ks[0], (B, S, D), dtype=jnp.float32), 'attention_mask': jnp.ones((B, S), dtype=jnp.int32), 'Wk': jax.random.normal(ks[1], (D, D), dtype=jnp.float32) * scale, 'bk': jnp.zeros((D,), dtype=jnp.float32), 'Wka': jax.random.normal(ks[2], (D, D), dtype=jnp.float32) * scale, 'bka': jnp.zeros((D,), dtype=jnp.float32), 'Wv': jax.random.normal(ks[3], (D, D), dtype=jnp.float32) * scale, 'bv': jnp.zeros((D,), dtype=jnp.float32), 'gamma': jnp.ones((D,), dtype=jnp.float32), 'beta': jnp.zeros((D,), dtype=jnp.float32)}
    _L1_attn_in = _L1_attn_setup()

    def _L1_ffn_setup():
        import jax, jax.numpy as jnp
        import numpy as np
        B, S, H, I, E, K = (4, 256, 128, 512, 4, 2)

        def _layer_norm(h, g, b, eps=1e-05):
            mu = h.mean(-1, keepdims=True)
            var = ((h - mu) ** 2).mean(-1, keepdims=True)
            return (h - mu) * jax.lax.rsqrt(var + eps) * g + b
        key = jax.random.key(seed)
        ks = jax.random.split(key, 24)
        rn = lambda k, shape, s=0.02: jax.random.normal(k, shape, dtype=jnp.float32) * s
        z = lambda shape: jnp.zeros(shape, jnp.float32)
        o = lambda shape: jnp.ones(shape, jnp.float32)
        return {'x': rn(ks[0], (B, S, H), 1.0), 'router_w': rn(ks[1], (H, E)), 'router_b': z((E,)), 'load_balancer': o((E,)), 'sw_w1': rn(ks[2], (H, I)), 'sw_w3': rn(ks[3], (H, I)), 'sw_w2': rn(ks[4], (I, H)), 'me_eq_w': rn(ks[5], (H, H)), 'me_eq_b': z((H,)), 'me_wv': rn(ks[6], (H, H)), 'me_bv': z((H,)), 'me_wo': rn(ks[7], (H, H)), 'me_bo': z((H,)), 'me_c1w': rn(ks[8], (H, 2 * H)), 'me_c1b': z((2 * H,)), 'me_c2w': rn(ks[9], (2 * H, H)), 'me_c2b': z((H,)), 'ce_syn_w': rn(ks[10], (H, H)), 'ce_syn_b': z((H,)), 'ce_wv': rn(ks[11], (H, H)), 'ce_bv': z((H,)), 'ce_wo': rn(ks[12], (H, H)), 'ce_bo': z((H,)), 'ce_n1g': o((H,)), 'ce_n1b': z((H,)), 'ce_f1w': rn(ks[13], (H, 2 * H)), 'ce_f1b': z((2 * H,)), 'ce_f2w': rn(ks[14], (2 * H, H)), 'ce_f2b': z((H,)), 'ce_n2g': o((H,)), 'ce_n2b': z((H,)), 'ce_gen_w': rn(ks[15], (H, H)), 'ce_gen_b': z((H,)), 'ml_w1': rn(ks[16], (H, I)), 'ml_b1': z((I,)), 'ml_w2': rn(ks[17], (I, H)), 'ml_b2': z((H,))}
    _L1_ffn_in = _L1_ffn_setup()

    def _L2_attn_setup():
        import math
        import jax, jax.numpy as jnp
        import numpy as np
        B, T, C = (2, 256, 128)
        H, N1, N2, N3 = (16, 6, 4, 6)
        HD = C // H

        def _rotary(T_, hd, dtype):
            inv_freq = 1.0 / 10000.0 ** (jnp.arange(0, hd, 2, dtype=jnp.float32) / hd)
            freqs = jnp.outer(jnp.arange(T_, dtype=jnp.float32), inv_freq)
            return (jnp.cos(freqs)[None, :, None, :].astype(dtype), jnp.sin(freqs)[None, :, None, :].astype(dtype))

        def _apply_rot(x, cos, sin):
            x1, x2 = (x[..., :x.shape[-1] // 2], x[..., x.shape[-1] // 2:])
            return jnp.concatenate([x1 * cos + x2 * sin, -x1 * sin + x2 * cos], axis=-1).astype(x.dtype)

        def _causal_bias(L, S, dtype):
            mask = jnp.triu(jnp.ones((L, S), bool), k=1)
            return jnp.where(mask, jnp.asarray(-jnp.inf, dtype), jnp.asarray(0.0, dtype))

        def _sdpa(q, k, v, scale):
            scores = jnp.einsum('bhtd,bhsd->bhts', q, k) * scale + _causal_bias(q.shape[-2], k.shape[-2], q.dtype)
            return jnp.einsum('bhts,bhsd->bhtd', jax.nn.softmax(scores, axis=-1), v)

        def _hyp_attn(q, k, v, curv):
            eps = 1e-06
            tq = jnp.sqrt(1.0 / curv + jnp.sum(q * q, axis=-1, keepdims=True))
            tk = jnp.sqrt(1.0 / curv + jnp.sum(k * k, axis=-1, keepdims=True))
            inner = jnp.einsum('bhtd,bhsd->bhts', q, k) - tq * jnp.swapaxes(tk, -1, -2)
            arg = jnp.maximum(-curv * inner, 1.0 + 1e-07)
            dis = jnp.sqrt(1.0 / curv) * jnp.arccosh(arg)
            scores = 1.0 / (eps + dis) + _causal_bias(q.shape[-2], k.shape[-2], q.dtype)
            return jnp.einsum('bhts,bhsd->bhtd', jax.nn.softmax(scores, axis=-1), v)
        key = jax.random.key(seed)
        k1, k2, k3 = jax.random.split(key, 3)
        return {'x': jax.random.normal(k1, (B, T, C), jnp.float32), 'qkv_w': jax.random.normal(k2, (3 * C, C), jnp.float32) * C ** (-0.5), 'proj_w': jax.random.normal(k3, (C, C), jnp.float32) * C ** (-0.5), 'proj_b': jnp.zeros((C,), jnp.float32), 'curvature': jnp.ones((1, N2, 1, 1), jnp.float32)}
    _L2_attn_in = _L2_attn_setup()

    def _L2_ffn_setup():
        import jax, jax.numpy as jnp
        import numpy as np
        key = jax.random.key(seed)
        kx, kw = jax.random.split(key)
        x = jax.random.normal(kx, (32, 512, 128), dtype=jnp.float32)
        weight = jax.random.normal(kw, (128, 128), dtype=jnp.float32) * 0.01
        return {'x': x, 'weight': weight}
    _L2_ffn_in = _L2_ffn_setup()

    def _L3_attn_setup():
        import jax, jax.numpy as jnp
        import numpy as np
        HEADS = 16
        HIDDEN = 128
        key = jax.random.key(seed)
        ks = jax.random.split(key, 9)
        E, H = (128, HIDDEN)
        N, L = (4, 256)
        s = 0.02
        return {'X_embed': jax.random.normal(ks[0], (N, L, E), dtype=jnp.float32), 'Wq': jax.random.normal(ks[1], (E, H), dtype=jnp.float32) * s, 'bq': jax.random.normal(ks[2], (H,), dtype=jnp.float32) * s, 'Wk': jax.random.normal(ks[3], (E, H), dtype=jnp.float32) * s, 'bk': jax.random.normal(ks[4], (H,), dtype=jnp.float32) * s, 'Wv': jax.random.normal(ks[5], (E, H), dtype=jnp.float32) * s, 'bv': jax.random.normal(ks[6], (H,), dtype=jnp.float32) * s, 'Wo': jax.random.normal(ks[7], (H, H), dtype=jnp.float32) * s, 'bo': jax.random.normal(ks[8], (H,), dtype=jnp.float32) * s}
    _L3_attn_in = _L3_attn_setup()

    def _L3_ffn_setup():
        import jax, jax.numpy as jnp
        import numpy as np
        B, T, DIM, H, DH, TOPK = (4, 256, 128, 8, 64, 3)
        key = jax.random.key(seed)
        ks = jax.random.split(key, 6)
        x = jax.random.normal(ks[0], (B, T, DIM), dtype=jnp.float32)
        sc = 1.0 / np.sqrt(DIM)
        Wq = jax.random.normal(ks[1], (DIM, H * DH), dtype=jnp.float32) * sc
        Wkv = jax.random.normal(ks[2], (DIM, 2 * H * DH), dtype=jnp.float32) * sc
        Ws = jax.random.normal(ks[3], (DIM, H), dtype=jnp.float32) * sc
        Wo = jax.random.normal(ks[4], (H, DH, DIM), dtype=jnp.float32) * (1.0 / np.sqrt(DH))
        bo = jax.random.normal(ks[5], (H, DIM), dtype=jnp.float32) * 0.01
        return {'x': x, 'Wq': Wq, 'Wkv': Wkv, 'Ws': Ws, 'Wo': Wo, 'bo': bo}
    _L3_ffn_in = _L3_ffn_setup()
    _d = {'L0_attn_hidden_states': _L0_attn_in['hidden_states'], 'L0_attn_in_proj_w': _L0_attn_in['in_proj_w'], 'L0_attn_conv_w': _L0_attn_in['conv_w'], 'L0_attn_conv_b': _L0_attn_in['conv_b'], 'L0_attn_x_proj_w': _L0_attn_in['x_proj_w'], 'L0_attn_dt_proj_w': _L0_attn_in['dt_proj_w'], 'L0_attn_dt_proj_b': _L0_attn_in['dt_proj_b'], 'L0_attn_dt_ln_w': _L0_attn_in['dt_ln_w'], 'L0_attn_b_ln_w': _L0_attn_in['b_ln_w'], 'L0_attn_c_ln_w': _L0_attn_in['c_ln_w'], 'L0_attn_A_log': _L0_attn_in['A_log'], 'L0_attn_D_skip': _L0_attn_in['D_skip'], 'L0_attn_out_proj_w': _L0_attn_in['out_proj_w'], 'L0_attn_input_ln_w': _L0_attn_in['input_ln_w'], 'L0_attn_pre_moe_ln_w': _L0_attn_in['pre_moe_ln_w'], 'L0_attn_gate_w': _L0_attn_in['gate_w'], 'L0_attn_up_w': _L0_attn_in['up_w'], 'L0_attn_down_w': _L0_attn_in['down_w'], 'L0_ffn_gate_w': _L0_ffn_in['gate_w'], 'L0_ffn_expert_gate': _L0_ffn_in['expert_gate'], 'L0_ffn_expert_up': _L0_ffn_in['expert_up'], 'L0_ffn_expert_down': _L0_ffn_in['expert_down'], 'L0_ffn_shared_gate_w': _L0_ffn_in['shared_gate_w'], 'L0_ffn_shared_up_w': _L0_ffn_in['shared_up_w'], 'L0_ffn_shared_down_w': _L0_ffn_in['shared_down_w'], 'L1_attn_attention_mask': _L1_attn_in['attention_mask'], 'L1_attn_Wk': _L1_attn_in['Wk'], 'L1_attn_bk': _L1_attn_in['bk'], 'L1_attn_Wka': _L1_attn_in['Wka'], 'L1_attn_bka': _L1_attn_in['bka'], 'L1_attn_Wv': _L1_attn_in['Wv'], 'L1_attn_bv': _L1_attn_in['bv'], 'L1_attn_gamma': _L1_attn_in['gamma'], 'L1_attn_beta': _L1_attn_in['beta'], 'L1_ffn_router_w': _L1_ffn_in['router_w'], 'L1_ffn_router_b': _L1_ffn_in['router_b'], 'L1_ffn_load_balancer': _L1_ffn_in['load_balancer'], 'L1_ffn_sw_w1': _L1_ffn_in['sw_w1'], 'L1_ffn_sw_w3': _L1_ffn_in['sw_w3'], 'L1_ffn_sw_w2': _L1_ffn_in['sw_w2'], 'L1_ffn_me_eq_w': _L1_ffn_in['me_eq_w'], 'L1_ffn_me_eq_b': _L1_ffn_in['me_eq_b'], 'L1_ffn_me_wv': _L1_ffn_in['me_wv'], 'L1_ffn_me_bv': _L1_ffn_in['me_bv'], 'L1_ffn_me_wo': _L1_ffn_in['me_wo'], 'L1_ffn_me_bo': _L1_ffn_in['me_bo'], 'L1_ffn_me_c1w': _L1_ffn_in['me_c1w'], 'L1_ffn_me_c1b': _L1_ffn_in['me_c1b'], 'L1_ffn_me_c2w': _L1_ffn_in['me_c2w'], 'L1_ffn_me_c2b': _L1_ffn_in['me_c2b'], 'L1_ffn_ce_syn_w': _L1_ffn_in['ce_syn_w'], 'L1_ffn_ce_syn_b': _L1_ffn_in['ce_syn_b'], 'L1_ffn_ce_wv': _L1_ffn_in['ce_wv'], 'L1_ffn_ce_bv': _L1_ffn_in['ce_bv'], 'L1_ffn_ce_wo': _L1_ffn_in['ce_wo'], 'L1_ffn_ce_bo': _L1_ffn_in['ce_bo'], 'L1_ffn_ce_n1g': _L1_ffn_in['ce_n1g'], 'L1_ffn_ce_n1b': _L1_ffn_in['ce_n1b'], 'L1_ffn_ce_f1w': _L1_ffn_in['ce_f1w'], 'L1_ffn_ce_f1b': _L1_ffn_in['ce_f1b'], 'L1_ffn_ce_f2w': _L1_ffn_in['ce_f2w'], 'L1_ffn_ce_f2b': _L1_ffn_in['ce_f2b'], 'L1_ffn_ce_n2g': _L1_ffn_in['ce_n2g'], 'L1_ffn_ce_n2b': _L1_ffn_in['ce_n2b'], 'L1_ffn_ce_gen_w': _L1_ffn_in['ce_gen_w'], 'L1_ffn_ce_gen_b': _L1_ffn_in['ce_gen_b'], 'L1_ffn_ml_w1': _L1_ffn_in['ml_w1'], 'L1_ffn_ml_b1': _L1_ffn_in['ml_b1'], 'L1_ffn_ml_w2': _L1_ffn_in['ml_w2'], 'L1_ffn_ml_b2': _L1_ffn_in['ml_b2'], 'L2_attn_qkv_w': _L2_attn_in['qkv_w'], 'L2_attn_proj_w': _L2_attn_in['proj_w'], 'L2_attn_proj_b': _L2_attn_in['proj_b'], 'L2_attn_curvature': _L2_attn_in['curvature'], 'L2_ffn_weight': _L2_ffn_in['weight'], 'L3_attn_Wq': _L3_attn_in['Wq'], 'L3_attn_bq': _L3_attn_in['bq'], 'L3_attn_Wk': _L3_attn_in['Wk'], 'L3_attn_bk': _L3_attn_in['bk'], 'L3_attn_Wv': _L3_attn_in['Wv'], 'L3_attn_bv': _L3_attn_in['bv'], 'L3_attn_Wo': _L3_attn_in['Wo'], 'L3_attn_bo': _L3_attn_in['bo'], 'L3_ffn_Wq': _L3_ffn_in['Wq'], 'L3_ffn_Wkv': _L3_ffn_in['Wkv'], 'L3_ffn_Ws': _L3_ffn_in['Ws'], 'L3_ffn_Wo': _L3_ffn_in['Wo'], 'L3_ffn_bo': _L3_ffn_in['bo']}
    _x0 = _d['L0_attn_hidden_states']
    _d['L0_attn_hidden_states'] = jax.random.normal(jax.random.fold_in(jax.random.key(seed), 1), (2, 2048, 128), dtype=_x0.dtype)
    del _x0
    return _d

def reference(L0_attn_hidden_states, L0_attn_in_proj_w, L0_attn_conv_w, L0_attn_conv_b, L0_attn_x_proj_w, L0_attn_dt_proj_w, L0_attn_dt_proj_b, L0_attn_dt_ln_w, L0_attn_b_ln_w, L0_attn_c_ln_w, L0_attn_A_log, L0_attn_D_skip, L0_attn_out_proj_w, L0_attn_input_ln_w, L0_attn_pre_moe_ln_w, L0_attn_gate_w, L0_attn_up_w, L0_attn_down_w, L0_ffn_gate_w, L0_ffn_expert_gate, L0_ffn_expert_up, L0_ffn_expert_down, L0_ffn_shared_gate_w, L0_ffn_shared_up_w, L0_ffn_shared_down_w, L1_attn_attention_mask, L1_attn_Wk, L1_attn_bk, L1_attn_Wka, L1_attn_bka, L1_attn_Wv, L1_attn_bv, L1_attn_gamma, L1_attn_beta, L1_ffn_router_w, L1_ffn_router_b, L1_ffn_load_balancer, L1_ffn_sw_w1, L1_ffn_sw_w3, L1_ffn_sw_w2, L1_ffn_me_eq_w, L1_ffn_me_eq_b, L1_ffn_me_wv, L1_ffn_me_bv, L1_ffn_me_wo, L1_ffn_me_bo, L1_ffn_me_c1w, L1_ffn_me_c1b, L1_ffn_me_c2w, L1_ffn_me_c2b, L1_ffn_ce_syn_w, L1_ffn_ce_syn_b, L1_ffn_ce_wv, L1_ffn_ce_bv, L1_ffn_ce_wo, L1_ffn_ce_bo, L1_ffn_ce_n1g, L1_ffn_ce_n1b, L1_ffn_ce_f1w, L1_ffn_ce_f1b, L1_ffn_ce_f2w, L1_ffn_ce_f2b, L1_ffn_ce_n2g, L1_ffn_ce_n2b, L1_ffn_ce_gen_w, L1_ffn_ce_gen_b, L1_ffn_ml_w1, L1_ffn_ml_b1, L1_ffn_ml_w2, L1_ffn_ml_b2, L2_attn_qkv_w, L2_attn_proj_w, L2_attn_proj_b, L2_attn_curvature, L2_ffn_weight, L3_attn_Wq, L3_attn_bq, L3_attn_Wk, L3_attn_bk, L3_attn_Wv, L3_attn_bv, L3_attn_Wo, L3_attn_bo, L3_ffn_Wq, L3_ffn_Wkv, L3_ffn_Ws, L3_ffn_Wo, L3_ffn_bo):

    def _L0_attn_ref(hidden_states, in_proj_w, conv_w, conv_b, x_proj_w, dt_proj_w, dt_proj_b, dt_ln_w, b_ln_w, c_ln_w, A_log, D_skip, out_proj_w, input_ln_w, pre_moe_ln_w, gate_w, up_w, down_w):
        import jax, jax.numpy as jnp
        import numpy as np
        D_MODEL = 128
        D_INNER = 256
        D_STATE = 16
        DT_RANK = 64
        K_CONV = 4
        D_FF = 512
        EPS = 1e-06

        def _rms(x, w):
            return x * jax.lax.rsqrt(jnp.mean(x * x, axis=-1, keepdims=True) + EPS) * w

        def _reference_tuple_inner(hidden_states, in_proj_w, conv_w, conv_b, x_proj_w, dt_proj_w, dt_proj_b, dt_ln_w, b_ln_w, c_ln_w, A_log, D_skip, out_proj_w, input_ln_w, pre_moe_ln_w, gate_w, up_w, down_w):
            B, S, _ = hidden_states.shape
            residual = hidden_states
            h = _rms(hidden_states, input_ln_w)
            xz = h @ in_proj_w
            x, z = jnp.split(xz, 2, axis=-1)
            xt = jnp.transpose(x, (0, 2, 1))
            conv_state = xt[:, :, -K_CONV:]
            y = jax.lax.conv_general_dilated(xt, conv_w[:, None, :], window_strides=(1,), padding=[(K_CONV - 1, 0)], feature_group_count=D_INNER, dimension_numbers=('NCH', 'OIH', 'NCH'))
            y = y + conv_b[None, :, None]
            x = jax.nn.silu(jnp.transpose(y, (0, 2, 1)))
            proj = x @ x_proj_w
            dt_raw = proj[..., :DT_RANK]
            B_raw = proj[..., DT_RANK:DT_RANK + D_STATE]
            C_raw = proj[..., DT_RANK + D_STATE:]
            dt = jax.nn.softplus(_rms(dt_raw, dt_ln_w) @ dt_proj_w + dt_proj_b)
            Bm = _rms(B_raw, b_ln_w)
            Cm = _rms(C_raw, c_ln_w)
            A = -jnp.exp(A_log)

            def step(hstate, ins):
                x_t, dt_t, B_t, C_t = ins
                dA = jnp.exp(dt_t[..., None] * A)
                hstate = hstate * dA + (dt_t * x_t)[..., None] * B_t[:, None, :]
                y_t = jnp.einsum('bdn,bn->bd', hstate, C_t)
                return (hstate, y_t)
            h0 = jnp.zeros((B, D_INNER, D_STATE), x.dtype)
            xs = (jnp.swapaxes(x, 0, 1), jnp.swapaxes(dt, 0, 1), jnp.swapaxes(Bm, 0, 1), jnp.swapaxes(Cm, 0, 1))
            ssm_state, ys = jax.lax.scan(step, h0, xs)
            y = jnp.swapaxes(ys, 0, 1) + x * D_skip
            y = y * jax.nn.silu(z)
            mamba_out = y @ out_proj_w
            hidden = residual + mamba_out
            residual = hidden
            hn = _rms(hidden, pre_moe_ln_w)
            ff = jax.nn.silu(hn @ gate_w) * (hn @ up_w) @ down_w
            out = residual + ff
            return (out, conv_state, ssm_state)
        return _reference_tuple_inner(hidden_states, in_proj_w, conv_w, conv_b, x_proj_w, dt_proj_w, dt_proj_b, dt_ln_w, b_ln_w, c_ln_w, A_log, D_skip, out_proj_w, input_ln_w, pre_moe_ln_w, gate_w, up_w, down_w)[0]

    def _L0_ffn_ref(hidden_states, gate_w, expert_gate, expert_up, expert_down, shared_gate_w, shared_up_w, shared_down_w):
        import jax, jax.numpy as jnp
        import numpy as np
        B, S, D = (4, 128, 128)
        I = 64
        E = 32
        TOP_K = 8
        N_GROUP = 8
        TOPK_GROUP = 4

        def _group_topk(scores):
            T = scores.shape[0]
            epg = E // N_GROUP
            group_scores = scores.reshape(T, N_GROUP, epg).sum(axis=-1)
            _, top_groups = jax.lax.top_k(group_scores, TOPK_GROUP)
            group_mask = jnp.zeros((T, N_GROUP), scores.dtype).at[jnp.arange(T)[:, None], top_groups].set(1.0)
            expert_mask = jnp.repeat(group_mask, epg, axis=1)
            masked_scores = scores * expert_mask
            topk_w, topk_i = jax.lax.top_k(masked_scores, TOP_K)
            return (topk_w, topk_i)

        def _reference_tuple_inner(hidden_states, gate_w, expert_gate, expert_up, expert_down, shared_gate_w, shared_up_w, shared_down_w):
            b, s, d = hidden_states.shape
            flat = hidden_states.reshape(-1, d)
            T = flat.shape[0]
            logits = flat @ gate_w.T
            scores = jax.nn.sigmoid(logits)
            topk_w, topk_i = _group_topk(scores)
            topk_w = topk_w / jnp.clip(topk_w.sum(axis=-1, keepdims=True), 1e-12)
            combine = jnp.zeros((T, E), flat.dtype).at[jnp.arange(T)[:, None], topk_i].add(topk_w)

            def body(acc, expert):
                wg, wu, wd, w = expert
                h = jax.nn.silu(flat @ wg.T) * (flat @ wu.T)
                return (acc + w[:, None] * (h @ wd.T), None)
            out, _ = jax.lax.scan(body, jnp.zeros_like(flat), (expert_gate, expert_up, expert_down, combine.T))
            shared = jax.nn.silu(flat @ shared_gate_w.T) * (flat @ shared_up_w.T) @ shared_down_w.T
            out = out + shared
            return (out.reshape(b, s, d), logits)
        return _reference_tuple_inner(hidden_states, gate_w, expert_gate, expert_up, expert_down, shared_gate_w, shared_up_w, shared_down_w)[0]

    def _L1_attn_ref(hidden_states, attention_mask, Wk, bk, Wka, bka, Wv, bv, gamma, beta):
        import jax, jax.numpy as jnp
        import numpy as np
        D = 128
        B = 4
        S = 512
        LN_EPS = 1e-05

        def _layer_norm(x, gamma, beta):
            mu = jnp.mean(x, axis=-1, keepdims=True)
            var = jnp.mean(jnp.square(x - mu), axis=-1, keepdims=True)
            return (x - mu) * jax.lax.rsqrt(var + LN_EPS) * gamma + beta
        h = _layer_norm(hidden_states, gamma, beta)
        d_model = h.shape[-1]
        keys = jnp.einsum('bsd,ed->bse', h, Wk) + bk
        values = jnp.einsum('bsd,ed->bse', h, Wv) + bv
        key_att = jnp.einsum('bsd,ed->bse', keys, Wka) + bka
        keys_weight = jnp.exp(key_att / jnp.sqrt(jnp.asarray(d_model, h.dtype)))
        keys_weight = keys_weight / jnp.cumsum(keys_weight, axis=1)
        pooled_keys = jnp.cumsum(keys_weight * keys, axis=1)
        return pooled_keys * values

    def _L1_ffn_ref(x, router_w, router_b, load_balancer, sw_w1, sw_w3, sw_w2, me_eq_w, me_eq_b, me_wv, me_bv, me_wo, me_bo, me_c1w, me_c1b, me_c2w, me_c2b, ce_syn_w, ce_syn_b, ce_wv, ce_bv, ce_wo, ce_bo, ce_n1g, ce_n1b, ce_f1w, ce_f1b, ce_f2w, ce_f2b, ce_n2g, ce_n2b, ce_gen_w, ce_gen_b, ml_w1, ml_b1, ml_w2, ml_b2):
        import jax, jax.numpy as jnp
        import numpy as np
        B, S, H, I, E, K = (4, 256, 128, 512, 4, 2)

        def _layer_norm(h, g, b, eps=1e-05):
            mu = h.mean(-1, keepdims=True)
            var = ((h - mu) ** 2).mean(-1, keepdims=True)
            return (h - mu) * jax.lax.rsqrt(var + eps) * g + b
        logits = jnp.einsum('bsh,he->bse', x, router_w) + router_b + load_balancer
        rw, sel = jax.lax.top_k(logits, K)
        rw = jax.nn.softmax(rw, axis=-1)
        e0 = jax.nn.silu(x @ sw_w1) * (x @ sw_w3) @ sw_w2
        eq = x @ me_eq_w + me_eq_b
        sym = (eq @ me_wv + me_bv) @ me_wo + me_bo
        e1 = jax.nn.gelu(sym @ me_c1w + me_c1b, approximate=False) @ me_c2w + me_c2b
        syn = x @ ce_syn_w + ce_syn_b
        attn = (syn @ ce_wv + ce_bv) @ ce_wo + ce_bo
        h2 = _layer_norm(syn + attn, ce_n1g, ce_n1b)
        ff = jax.nn.relu(h2 @ ce_f1w + ce_f1b) @ ce_f2w + ce_f2b
        h2 = _layer_norm(h2 + ff, ce_n2g, ce_n2b)
        e2 = h2 @ ce_gen_w + ce_gen_b
        e3 = jax.nn.gelu(x @ ml_w1 + ml_b1, approximate=False) @ ml_w2 + ml_b2
        stack = jnp.stack([e0, e1, e2, e3], axis=2)
        gathered = jnp.take_along_axis(stack, sel[..., None], axis=2)
        return (rw[..., None] * gathered).sum(axis=2)

    def _L2_attn_ref(x, qkv_w, proj_w, proj_b, curvature):
        import math
        import jax, jax.numpy as jnp
        import numpy as np
        B, T, C = (2, 256, 128)
        H, N1, N2, N3 = (16, 6, 4, 6)
        HD = C // H

        def _rotary(T_, hd, dtype):
            inv_freq = 1.0 / 10000.0 ** (jnp.arange(0, hd, 2, dtype=jnp.float32) / hd)
            freqs = jnp.outer(jnp.arange(T_, dtype=jnp.float32), inv_freq)
            return (jnp.cos(freqs)[None, :, None, :].astype(dtype), jnp.sin(freqs)[None, :, None, :].astype(dtype))

        def _apply_rot(x, cos, sin):
            x1, x2 = (x[..., :x.shape[-1] // 2], x[..., x.shape[-1] // 2:])
            return jnp.concatenate([x1 * cos + x2 * sin, -x1 * sin + x2 * cos], axis=-1).astype(x.dtype)

        def _causal_bias(L, S, dtype):
            mask = jnp.triu(jnp.ones((L, S), bool), k=1)
            return jnp.where(mask, jnp.asarray(-jnp.inf, dtype), jnp.asarray(0.0, dtype))

        def _sdpa(q, k, v, scale):
            scores = jnp.einsum('bhtd,bhsd->bhts', q, k) * scale + _causal_bias(q.shape[-2], k.shape[-2], q.dtype)
            return jnp.einsum('bhts,bhsd->bhtd', jax.nn.softmax(scores, axis=-1), v)

        def _hyp_attn(q, k, v, curv):
            eps = 1e-06
            tq = jnp.sqrt(1.0 / curv + jnp.sum(q * q, axis=-1, keepdims=True))
            tk = jnp.sqrt(1.0 / curv + jnp.sum(k * k, axis=-1, keepdims=True))
            inner = jnp.einsum('bhtd,bhsd->bhts', q, k) - tq * jnp.swapaxes(tk, -1, -2)
            arg = jnp.maximum(-curv * inner, 1.0 + 1e-07)
            dis = jnp.sqrt(1.0 / curv) * jnp.arccosh(arg)
            scores = 1.0 / (eps + dis) + _causal_bias(q.shape[-2], k.shape[-2], q.dtype)
            return jnp.einsum('bhts,bhsd->bhtd', jax.nn.softmax(scores, axis=-1), v)
        Bx, Tx, Cx = x.shape
        qkv = x @ qkv_w.T
        q, k, v = jnp.split(qkv, 3, axis=-1)
        q = q.reshape(Bx, Tx, H, HD)
        k = k.reshape(Bx, Tx, H, HD)
        v = v.reshape(Bx, Tx, H, HD)
        cos, sin = _rotary(Tx, HD, x.dtype)
        q = _apply_rot(q, cos, sin)
        k = _apply_rot(k, cos, sin)
        q, k, v = (jnp.swapaxes(t, 1, 2) for t in (q, k, v))
        outs = []
        outs.append(_sdpa(q[:, :N1], k[:, :N1], v[:, :N1], 1.0 / math.sqrt(HD)))
        outs.append(_hyp_attn(q[:, N1:N1 + N2], k[:, N1:N1 + N2], v[:, N1:N1 + N2], curvature))
        qn = q[:, N1 + N2:] / jnp.maximum(jnp.linalg.norm(q[:, N1 + N2:], axis=-1, keepdims=True), 1e-12)
        kn = k[:, N1 + N2:] / jnp.maximum(jnp.linalg.norm(k[:, N1 + N2:], axis=-1, keepdims=True), 1e-12)
        outs.append(_sdpa(qn, kn, v[:, N1 + N2:], math.sqrt(HD)))
        y = jnp.concatenate(outs, axis=1)
        y = jnp.swapaxes(y, 1, 2).reshape(Bx, Tx, Cx)
        return y @ proj_w.T + proj_b

    def _L2_ffn_ref(x, weight):
        import jax, jax.numpy as jnp
        import numpy as np
        b_weight = jnp.sign(weight)
        return jnp.einsum('bsi,oi->bso', x, b_weight)

    def _L3_attn_ref(X_embed, Wq, bq, Wk, bk, Wv, bv, Wo, bo):
        import jax, jax.numpy as jnp
        import numpy as np
        HEADS = 16
        HIDDEN = 128
        N, L, _ = X_embed.shape
        H, heads = (HIDDEN, HEADS)
        dh = H // heads
        Q = X_embed @ Wq + bq
        K = X_embed @ Wk + bk
        V = X_embed @ Wv + bv
        Q = Q.reshape(N, heads, L, dh)
        K = K.reshape(N, heads, L, dh)
        V = V.reshape(N, heads, L, dh)
        scale = np.float32(1.0 / np.sqrt(H))
        Q = Q * scale
        K = K * scale
        scores = jnp.einsum('neax,nebx->neab', Q, K)
        A = jax.nn.softmax(scores, axis=2)
        Out = jnp.einsum('neab,neax->neax', A, V)
        Out = Out.reshape(N, L, H)
        return Out @ Wo + bo

    def _L3_ffn_ref(x, Wq, Wkv, Ws, Wo, bo):
        import jax, jax.numpy as jnp
        import numpy as np
        B, T, DIM, H, DH, TOPK = (4, 256, 128, 8, 64, 3)
        b, t, _ = x.shape
        s = jax.nn.sigmoid(x @ Ws)
        vals, idx = jax.lax.top_k(s, TOPK)
        bi = jnp.arange(b)[:, None, None]
        ti = jnp.arange(t)[None, :, None]
        scores = jnp.zeros_like(s).at[bi, ti, idx].set(vals)
        q = (x @ Wq).reshape(b, t, H, DH).transpose(0, 2, 1, 3)
        kv = (x @ Wkv).reshape(b, t, 2, H, DH).transpose(2, 0, 3, 1, 4)
        k, v = (kv[0], kv[1])
        scale = DH ** (-0.5)
        attn = jax.nn.softmax(jnp.einsum('bhid,bhjd->bhij', q * scale, k), axis=-1)
        out = jnp.einsum('bhij,bhjd->bhid', attn, v)
        proj = jnp.einsum('bhtd,hde->bhte', out, Wo) + bo[None, :, None, :]
        return jnp.einsum('bhte,bth->bte', proj, scores)
    x = L0_attn_hidden_states
    xn = _layernorm(x, axis=-1)
    x = x + _L0_attn_ref(xn, L0_attn_in_proj_w, L0_attn_conv_w, L0_attn_conv_b, L0_attn_x_proj_w, L0_attn_dt_proj_w, L0_attn_dt_proj_b, L0_attn_dt_ln_w, L0_attn_b_ln_w, L0_attn_c_ln_w, L0_attn_A_log, L0_attn_D_skip, L0_attn_out_proj_w, L0_attn_input_ln_w, L0_attn_pre_moe_ln_w, L0_attn_gate_w, L0_attn_up_w, L0_attn_down_w) + _L0_ffn_ref(xn, L0_ffn_gate_w, L0_ffn_expert_gate, L0_ffn_expert_up, L0_ffn_expert_down, L0_ffn_shared_gate_w, L0_ffn_shared_up_w, L0_ffn_shared_down_w)
    xn = _layernorm(x, axis=-1)
    x = x + _L1_attn_ref(xn, L1_attn_attention_mask, L1_attn_Wk, L1_attn_bk, L1_attn_Wka, L1_attn_bka, L1_attn_Wv, L1_attn_bv, L1_attn_gamma, L1_attn_beta) + _L1_ffn_ref(xn, L1_ffn_router_w, L1_ffn_router_b, L1_ffn_load_balancer, L1_ffn_sw_w1, L1_ffn_sw_w3, L1_ffn_sw_w2, L1_ffn_me_eq_w, L1_ffn_me_eq_b, L1_ffn_me_wv, L1_ffn_me_bv, L1_ffn_me_wo, L1_ffn_me_bo, L1_ffn_me_c1w, L1_ffn_me_c1b, L1_ffn_me_c2w, L1_ffn_me_c2b, L1_ffn_ce_syn_w, L1_ffn_ce_syn_b, L1_ffn_ce_wv, L1_ffn_ce_bv, L1_ffn_ce_wo, L1_ffn_ce_bo, L1_ffn_ce_n1g, L1_ffn_ce_n1b, L1_ffn_ce_f1w, L1_ffn_ce_f1b, L1_ffn_ce_f2w, L1_ffn_ce_f2b, L1_ffn_ce_n2g, L1_ffn_ce_n2b, L1_ffn_ce_gen_w, L1_ffn_ce_gen_b, L1_ffn_ml_w1, L1_ffn_ml_b1, L1_ffn_ml_w2, L1_ffn_ml_b2)
    xn = _layernorm(x, axis=-1)
    x = x + _L2_attn_ref(xn, L2_attn_qkv_w, L2_attn_proj_w, L2_attn_proj_b, L2_attn_curvature) + _L2_ffn_ref(xn, L2_ffn_weight)
    xn = _layernorm(x, axis=-1)
    x = x + _L3_attn_ref(xn, L3_attn_Wq, L3_attn_bq, L3_attn_Wk, L3_attn_bk, L3_attn_Wv, L3_attn_bv, L3_attn_Wo, L3_attn_bo) + _L3_ffn_ref(xn, L3_ffn_Wq, L3_ffn_Wkv, L3_ffn_Ws, L3_ffn_Wo, L3_ffn_bo)
    return x

_drawn_inputs = setup_inputs


def setup_inputs(seed=0):
    import zlib

    import numpy as np

    out = dict(_drawn_inputs(seed))
    spreads = {'L0_attn_conv_b': (0.0, 0.1),
     'L0_attn_dt_proj_b': (-2.0, 0.2),
     'L0_attn_dt_ln_w': (1.0, 0.2),
     'L0_attn_b_ln_w': (1.0, 0.2),
     'L0_attn_c_ln_w': (1.0, 0.544),
     'L0_attn_D_skip': (1.0, 0.2),
     'L0_attn_input_ln_w': (1.0, 0.2),
     'L0_attn_pre_moe_ln_w': (1.0, 0.2),
     'L1_attn_bk': (0.0, 0.1),
     'L1_attn_bka': (0.0, 2.0),
     'L1_attn_bv': (0.0, 0.1),
     'L1_attn_gamma': (1.0, 0.2),
     'L1_attn_beta': (0.0, 0.1),
     'L1_ffn_router_b': (0.0, 0.661),
     'L1_ffn_load_balancer': (1.0, 0.2),
     'L1_ffn_me_eq_b': (0.0, 0.8),
     'L1_ffn_me_bv': (0.0, 0.8),
     'L1_ffn_me_bo': (0.0, 0.8),
     'L1_ffn_me_c1b': (0.0, 0.8),
     'L1_ffn_me_c2b': (0.0, 0.8),
     'L1_ffn_ce_syn_b': (0.0, 0.621),
     'L1_ffn_ce_bv': (0.0, 0.8),
     'L1_ffn_ce_bo': (0.0, 0.427),
     'L1_ffn_ce_n1g': (1.0, 0.6),
     'L1_ffn_ce_n1b': (0.0, 0.8),
     'L1_ffn_ce_f1b': (0.0, 0.8),
     'L1_ffn_ce_f2b': (0.0, 0.8),
     'L1_ffn_ce_n2g': (1.0, 0.6),
     'L1_ffn_ce_n2b': (0.0, 0.8),
     'L1_ffn_ce_gen_b': (0.0, 0.461),
     'L1_ffn_ml_b1': (0.0, 0.8),
     'L1_ffn_ml_b2': (0.0, 0.618),
     'L2_attn_proj_b': (0.0, 0.8),
     'L2_attn_curvature': (1.0, 0.6)}
    factors = {'L0_ffn_gate_w': 8.0,
     'L0_ffn_expert_gate': 8.0,
     'L0_ffn_expert_up': 8.0,
     'L0_ffn_expert_down': 8.0,
     'L0_ffn_shared_gate_w': 8.0,
     'L0_ffn_shared_up_w': 8.0,
     'L0_ffn_shared_down_w': 8.0,
     'L1_ffn_router_w': 3.424,
     'L1_ffn_sw_w1': 8.0,
     'L1_ffn_sw_w3': 8.0,
     'L1_ffn_sw_w2': 8.0,
     'L1_ffn_me_eq_w': 8.0,
     'L1_ffn_me_wv': 8.0,
     'L1_ffn_me_wo': 8.0,
     'L1_ffn_me_c1w': 8.0,
     'L1_ffn_me_c2w': 8.0,
     'L1_ffn_ce_wv': 8.0,
     'L1_ffn_ce_wo': 8.0,
     'L1_ffn_ce_f1w': 8.0,
     'L1_ffn_ce_f2w': 8.0,
     'L1_ffn_ml_w1': 7.913,
     'L1_ffn_ml_w2': 6.946,
     'L2_attn_qkv_w': 4.761,
     'L2_attn_proj_w': 4.328,
     'L3_attn_Wq': 64.0,
     'L3_attn_bq': 64.0,
     'L3_attn_Wk': 64.0,
     'L3_attn_bk': 64.0,
     'L3_attn_Wv': 8.0,
     'L3_attn_bv': 30.394,
     'L3_attn_Wo': 8.0,
     'L3_attn_bo': 62.157,
     'L3_ffn_Wq': 3.408,
     'L3_ffn_Wkv': 3.023,
     'L3_ffn_Ws': 3.842,
     'L3_ffn_Wo': 2.988,
     'L3_ffn_bo': 64.0}
    for name, (base, spread) in spreads.items():
        noise = np.random.default_rng([zlib.crc32(name.encode()), seed]).standard_normal(out[name].shape)
        drawn = base * np.exp(spread * noise) if base else spread * noise
        out[name] = jnp.asarray(drawn.astype(out[name].dtype))
    for name, factor in factors.items():
        out[name] = (out[name] * factor).astype(out[name].dtype)
    return out
```

```python
from contextlib import ExitStack, contextmanager

import numpy as np
import concourse.bass as bass
from concourse import mybir

F32 = mybir.dt.float32
BF16 = mybir.dt.bfloat16
ALU = mybir.AluOpType
ACT = mybir.ActivationFunctionType
AX = mybir.AxisListType

B, S, D = 2, 2048, 128
T = B * S
CH = 512
NC = T // CH
CPB = S // CH
NT = T // 128
D_INNER, D_STATE, DT_RANK, K_CONV = 256, 16, 64, 4
NE0 = 32


class Pack:

    def __init__(self, items):
        self.at, n = {}, 0
        for name, rows, cols in items:
            self.at[name] = (n, rows, cols)
            n += cols
        self.n = n

    def view(self, tile, name):
        o, rows, cols = self.at[name]
        return tile[0:rows, o:o + cols]

    def fill(self, parts):
        out = np.zeros((128, self.n), np.float32)
        for name, (o, rows, cols) in self.at.items():
            out[0:rows, o:o + cols] = np.asarray(parts[name]).reshape(rows, cols)
        return out


PACKS = {
    "c": Pack([("ones", 128, 128), ("ones64", 64, 128), ("bcmean", 96, 96), ("ident", 128, 128),
               ("eps5", 128, 1), ("eps6", 128, 1), ("one", 128, 1), ("minus_one", 128, 1), ("minus_inv_d", 128, 1), ("tri8", 128, 64), ("tri4", 128, 16)]),
    "m": Pack([("in_proj", 128, 512), ("conv_w", 128, 8), ("conv_b", 128, 2), ("xp_dt", 128, 128),
               ("xp_bc", 128, 192), ("dt_proj", 64, 256), ("dt_b", 128, 2), ("dt_ln", 64, 1),
               ("bc_ln", 96, 1), ("A_log", 128, 32), ("D_skip", 128, 2), ("out_proj", 128, 256),
               ("in_ln", 128, 1), ("ff_ln", 128, 1)]),
    "f": Pack([("gate", 128, 512), ("up", 128, 512), ("down", 128, 512)]),
    "l1": Pack([(n, 128, 128) for n in ("Wk", "Wka", "Wv", "ce_syn", "ce_synT", "ce_wv", "ce_wo", "me_eqT", "me_wv", "me_wo",
                                        "gen", "ones_row")] + [
        (n, 128, 1) for n in ("bk", "bka", "bv", "gamma", "beta", "me_eqb", "me_bv", "me_bo", "me_c2b", "ce_synb", "ce_bv",
                              "ce_bo", "n1g", "n1b", "f2b", "n2g", "n2b", "gen_b", "ml_b2")] + [
        ("router", 128, 4), ("router_b", 1, 4), ("balancer", 1, 4), ("me_c1", 128, 256), ("me_c1b", 128, 2),
        ("me_c2", 128, 256), ("f1", 128, 256), ("f1b", 128, 2), ("f2", 128, 256), ("sw1", 128, 512), ("sw3", 128, 512),
        ("sw2", 128, 512), ("ml1", 128, 512), ("ml_b1", 128, 4), ("ml2", 128, 512)]),
    "l2": Pack([(n, 128, 128) for n in ("Wq", "Wqs", "Wk", "Wks", "Wv", "Wo", "bin", "blocks8", "seen")] + [
        (n, 128, 1) for n in ("c", "inv_c", "hyp", "q_base", "q_cos", "k_base", "k_cos", "root_inv_c", "proj_b")] + [
        ("hyp_c", 128, 4), ("hyp_root", 128, 4)]),
    "l3": Pack([(n, 128, 128) for n in ("Wq", "Wk", "Wv", "Wo")] + [(n, 128, 1) for n in ("bq", "bk", "bv", "bo")] + [
        ("FWq", 128, 512), ("FWk", 128, 512), ("FWv", 128, 512), ("Ws", 128, 8), ("wo2", 128, 1024), ("bo3", 8, 128)]),
    "e": Pack([("router", 128, NE0), ("gate", 128, 2048), ("up", 128, 2048), ("down", 128, 2048),
               ("sgate", 128, 64), ("sup", 128, 64), ("sdown", 64, 128)]),
}


class Scope:
    RECYCLE = 80
    ended = []

    def __init__(self, nc, name):
        self.nc, self.name, self.stack, self.sems = nc, name, ExitStack(), []

    def __enter__(self):
        return self

    def __exit__(self, *err):
        self.stack.close()
        Scope.ended += self.sems
        if len(Scope.ended) >= self.RECYCLE:
            self.nc.clear_and_free_semaphores(Scope.ended)
            self.nc.all_engine_barrier()
            Scope.ended = []

    def sb(self, name, shape, dt=F32):
        return self.stack.enter_context(self.nc.sbuf_tensor(f"{self.name}_{name}", shape, dt))

    def ps(self, name, shape, dt=F32):
        return self.stack.enter_context(self.nc.psum_tensor(f"{self.name}_{name}", shape, dt))

    def sem(self, name):
        self.sems.append(self.nc.alloc_semaphore(f"{self.name}_{name}"))
        return self.sems[-1]


def wait(eng, sem, value, alone=None):
    eng.wait_ge(sem, value)
    if alone is not None:
        eng.sem_inc(alone, 1)


class Steps:

    def __init__(self, eng, sem):
        self.eng, self.sem, self.base, self.k = eng, sem, 0, 0

    def __call__(self, ins):
        ins.then_inc(self.sem, 1)
        self.k += 1
        wait(self.eng, self.sem, self.base + self.k)

    @contextmanager
    def loop(self, n, per):
        base = self.base + self.k
        with self.eng.Fori(0, n) as i:
            self.base, self.k = base + i * per, 0
            yield i
            assert self.k == per, (self.k, per)
        self.base, self.k = base + n * per, 0


def load(nc, name, pairs):
    with Scope(nc, name) as sc:
        loaded = sc.sem("loaded")
        with nc.Block() as block:
            @block.sync
            def _(sp):
                for dst, src in pairs:
                    sp.dma_start(dst, src).then_inc(loaded, 16)
                sp.wait_ge(loaded, 16 * len(pairs))


def cols(tile, c, n=CH):
    return tile[:, bass.ts(c, n)]


def norm(nc, name, src, dst, mean_w, eps, center=True, gain=None, shift=None, rows=128):
    with Scope(nc, name) as sc:
        sq = sc.sb("sq", [rows, T])
        rstd = sc.sb("rstd", [rows, T])
        ps = sc.ps("ps", [128, NC * CH])
        mean_ready, centred, squared = sc.sem("mean_ready"), sc.sem("centred"), sc.sem("squared")
        var_ready, ln_done, rstd_ready = sc.sem("var_ready"), sc.sem("ln_done"), sc.sem("rstd_ready")
        normed, scaled = sc.sem("normed"), sc.sem("scaled")
        act_waits, dve_waits = sc.sem("act_waits"), sc.sem("dve_waits")
        acc = ps[0:rows, :]
        with nc.Block() as block:
            @block.tensor
            def _(pe):
                if center:
                    with pe.Fori(0, NC) as c:
                        pe.matmul(cols(ps[0:mean_w.shape[1], :], c), mean_w, cols(src, c), start=True, stop=True).then_inc(mean_ready, 1)
                with pe.Fori(0, NC) as c:
                    wait(pe, squared, c + 1)
                    pe.matmul(cols(ps[0:mean_w.shape[1], :], c), mean_w, cols(sq, c), start=True, stop=True).then_inc(var_ready, 1)

            @block.scalar
            def _(act):
                act.preload_act_table_set("natural_log_exp_and_others")
                with act.Fori(0, NC) as c:
                    if center:
                        wait(act, centred, c + 1)
                    act.activation(cols(sq, c), cols(dst if center else src, c), ACT.Square).then_inc(squared, 1)
                with act.Fori(0, NC) as c:
                    wait(act, var_ready, c + 1)
                    act.activation(cols(rstd, c), cols(acc, c), ACT.Ln, bias=eps[0:rows, :]).then_inc(ln_done, 1)
                    wait(act, ln_done, c + 1, act_waits)
                    act.activation(cols(rstd, c), cols(rstd, c), ACT.Exp, scale=-0.5).then_inc(rstd_ready, 1)

            @block.vector
            def _(dve):
                if center:
                    with dve.Fori(0, NC) as c:
                        wait(dve, mean_ready, c + 1)
                        dve.tensor_tensor(cols(dst, c), cols(src, c), cols(acc, c), ALU.subtract).then_inc(centred, 1)
                with dve.Fori(0, NC) as c:
                    wait(dve, rstd_ready, c + 1)
                    base = dst if center else src
                    if gain is not None and shift is None:
                        dve.scalar_tensor_tensor(out=cols(dst, c), in0=cols(base, c), scalar=gain, in1=cols(rstd, c),
                                                 op0=ALU.mult, op1=ALU.mult).then_inc(normed, 1)
                    else:
                        dve.tensor_tensor(cols(dst, c), cols(base, c), cols(rstd, c), ALU.mult).then_inc(normed, 1)
                    if shift is not None:
                        wait(dve, normed, c + 1)
                        dve.tensor_scalar(cols(dst, c), cols(dst, c), gain, shift, ALU.mult, ALU.add).then_inc(scaled, 1)


def linear(nc, name, jobs):
    with Scope(nc, name) as sc:
        ps = sc.ps("ps", [128, NC * CH])
        ready, act_done, dve_done = sc.sem("ready"), sc.sem("act_done"), sc.sem("dve_done")
        counts = {"act": 0, "dve": 0}
        before = []
        for job in jobs:
            before.append(counts[job["by"]])
            counts[job["by"]] += NC
        done = {"act": act_done, "dve": dve_done}

        def rows(job):
            return job["terms"][0][0].shape[1]

        def place(job, b, k):
            pad = job.get("pad", 0)
            return job["dst"][:, bass.ds(b * (S + pad) + k * CH + pad, CH)]

        with nc.Block() as block:
            @block.tensor
            def _(pe):
                for j, job in enumerate(jobs):
                    with pe.Fori(0, NC) as c:
                        if j:
                            wait(pe, done[jobs[j - 1]["by"]], c + before[j - 1] + 1)
                        n = len(job["terms"])
                        for i, (w, src) in enumerate(job["terms"]):
                            mm = pe.matmul(cols(ps[0:rows(job), :], c), w, cols(src, c), start=(i == 0), stop=(i == n - 1))
                        mm.then_inc(ready, 1)

            @block.scalar
            def _(act):
                for j, job in enumerate(jobs):
                    if job["by"] != "act":
                        continue
                    with act.Fori(0, B) as b:
                        with act.Fori(0, CPB) as k:
                            wait(act, ready, b * CPB + k + (j * NC + 1))
                            act.activation(place(job, b, k), ps[0:rows(job), bass.ds(b * S + k * CH, CH)],
                                           job.get("func", ACT.Identity), bias=job.get("bias", 0.0),
                                           scale=job.get("scale", 1.0)).then_inc(act_done, 1)

            @block.vector
            def _(dve):
                for j, job in enumerate(jobs):
                    if job["by"] != "dve":
                        continue
                    with dve.Fori(0, B) as b:
                        with dve.Fori(0, CPB) as k:
                            wait(dve, ready, b * CPB + k + (j * NC + 1))
                            bank = ps[0:rows(job), bass.ds(b * S + k * CH, CH)]
                            if "add" in job and "bias" in job:
                                ins = dve.scalar_tensor_tensor(out=place(job, b, k), in0=bank, scalar=job["bias"],
                                                               in1=job["add"][:, bass.ds(b * S + k * CH, CH)],
                                                               op0=ALU.add, op1=ALU.add)
                            elif "add" in job:
                                ins = dve.tensor_tensor(place(job, b, k), bank,
                                                        job["add"][:, bass.ds(b * S + k * CH, CH)], ALU.add)
                            elif "bias" in job:
                                ins = dve.tensor_scalar(place(job, b, k), bank, job["bias"], None, ALU.add)
                            else:
                                ins = dve.tensor_copy(place(job, b, k), bank)
                            ins.then_inc(dve_done, 1)


def expert_blocks(nc, name, src, blocks, weights, dst, resid, bias=None):
    nb = len(blocks)
    m = [b["gate"].shape[1] for b in blocks]
    twice = [b.get("up") is not None and b.get("sel") is not None for b in blocks]
    with Scope(nc, name) as sc:
        g_ps, u_ps = sc.ps("g_ps", [128, 2, CH]), sc.ps("u_ps", [128, 2, CH])
        w_ps, o_ps = sc.ps("w_ps", [128, 2, CH]), sc.ps("o_ps", [128, CH])
        g_sb, h_sb = sc.sb("g_sb", [128, 2, CH]), sc.sb("h_sb", [128, 2, CH])
        gate_ready, factors_ready = sc.sem("gate_ready"), sc.sem("factors_ready")
        act_done, hid_done, own = sc.sem("act_done"), sc.sem("hid_done"), sc.sem("dve_step")
        down_done, out_free, pe_waits = sc.sem("down_done"), sc.sem("out_free"), sc.sem("pe_waits")
        with nc.Block() as block:
            @block.tensor
            def _(pe):
                def down(c, j):
                    wait(pe, hid_done, c * nb + (j + 1))
                    if j == 0:
                        wait(pe, out_free, c + 1)
                    pe.matmul(o_ps[:, :], blocks[j]["down"], h_sb[0:m[j], j % 2, :], start=(j == 0),
                              stop=(j == nb - 1)).then_inc(down_done, 1)

                with pe.Fori(0, NC) as c:
                    for j, blk in enumerate(blocks):
                        if j >= 2:
                            wait(pe, hid_done, c * nb + (j - 1), pe_waits if m[j] < 128 else None)
                        pe.matmul(g_ps[0:m[j], j % 2, :], blk["gate"], cols(src, c), start=True, stop=True).then_inc(gate_ready, 1)
                        if blk.get("up") is not None:
                            last = pe.matmul(u_ps[0:m[j], j % 2, :], blk["up"], cols(src, c), start=True, stop=True)
                        if blk.get("sel") is not None:
                            last = pe.matmul(w_ps[0:m[j], j % 2, :], blk["sel"], cols(weights, c), start=True, stop=True)
                        last.then_inc(factors_ready, 1)
                        if j:
                            down(c, j - 1)
                    down(c, nb - 1)

            @block.scalar
            def _(act):
                with act.Fori(0, NC) as c:
                    for j, blk in enumerate(blocks):
                        wait(act, gate_ready, c * nb + (j + 1))
                        if j >= 2:
                            wait(act, hid_done, c * nb + (j - 1))
                        act.activation(g_sb[0:m[j], j % 2, :], g_ps[0:m[j], j % 2, :], blk["func"],
                                       bias=blk.get("bias", 0.0)).then_inc(act_done, 1)

            @block.vector
            def _(dve):
                dve.sem_inc(out_free, 1)
                steps = Steps(dve, own)
                with steps.loop(NC, sum(twice) + (bias is not None)) as c:
                    for j, blk in enumerate(blocks):
                        wait(dve, act_done, c * nb + (j + 1))
                        wait(dve, factors_ready, c * nb + (j + 1))
                        if j >= 2:
                            wait(dve, down_done, c * nb + (j - 1))
                        g, u = g_sb[0:m[j], j % 2, :], u_ps[0:m[j], j % 2, :]
                        w, h = w_ps[0:m[j], j % 2, :], h_sb[0:m[j], j % 2, :]
                        if twice[j]:
                            steps(dve.tensor_tensor(g, g, u, ALU.mult))
                        other = w if blk.get("sel") is not None else u
                        dve.tensor_tensor(h, g, other, ALU.mult).then_inc(hid_done, 1)
                    wait(dve, down_done, c * nb + nb)
                    if bias is not None:
                        steps(dve.tensor_scalar(cols(dst, c), cols(resid, c), bias, None, ALU.add))
                        dve.tensor_tensor(cols(dst, c), o_ps[:, :], cols(dst, c), ALU.add).then_inc(out_free, 1)
                    else:
                        dve.tensor_tensor(cols(dst, c), o_ps[:, :], cols(resid, c), ALU.add).then_inc(out_free, 1)



SEG = 1024


def conv_silu(nc, xpre, xs, w, bias):
    pad = K_CONV - 1
    with Scope(nc, "conv") as sc:
        conv_done, own = sc.sem("conv_done"), sc.sem("dve_step")
        silu_done = sc.sem("silu_done")
        with nc.Block() as block:
            @block.vector
            def _(dve):
                steps = Steps(dve, own)
                for h in range(2):
                    for b in range(B):
                        x = xpre[:, h, b * (S + pad):(b + 1) * (S + pad)]
                        y = xs[:, h, b * S:(b + 1) * S]
                        steps(dve.tensor_scalar(y, x[:, 0:S], w[:, 4 * h:4 * h + 1], bias[:, h:h + 1], ALU.mult, ALU.add))
                        for k in (1, 2):
                            steps(dve.scalar_tensor_tensor(out=y, in0=x[:, k:k + S], scalar=w[:, 4 * h + k:4 * h + k + 1],
                                                           in1=y, op0=ALU.mult, op1=ALU.add))
                        dve.scalar_tensor_tensor(out=y, in0=x[:, 3:3 + S], scalar=w[:, 4 * h + 3:4 * h + 4],
                                                 in1=y, op0=ALU.mult, op1=ALU.add).then_inc(conv_done, 1)

            @block.scalar
            def _(act):
                for n in range(2 * B):
                    wait(act, conv_done, n + 1)
                    y = xs[:, n // B, (n % B) * S:(n % B + 1) * S]
                    act.activation(y, y, ACT.Silu).then_inc(silu_done, 1)


def split3(nc, name, src, dst, rows, part):
    with Scope(nc, name) as sc:
        hi, r1, mid = sc.sb("hi", [rows, T], BF16), sc.sb("r1", [rows, T]), sc.sb("mid", [rows, T], BF16)
        own = sc.sem("dve_step")
        with nc.Block() as block:
            @block.vector
            def _(dve):
                steps = Steps(dve, own)
                steps(dve.tensor_copy(hi[:, :], src))
                steps(dve.tensor_tensor(r1[:, :], src, hi[:, :], ALU.subtract))
                steps(dve.tensor_copy(mid[:, :], r1[:, :]))
                steps(dve.tensor_tensor(r1[:, :], r1[:, :], mid[:, :], ALU.subtract))
                steps(dve.tensor_copy(dst[0:32, :], hi[0:32, :]))
                steps(dve.tensor_copy(dst[32:64, :], mid[32:64, :]))
                steps(dve.tensor_copy(dst[64:96, :], r1[64:96, :]))


def softplus(nc, pre, tmp):
    with Scope(nc, "softplus") as sc:
        own, ln_done, dve_done = sc.sem("act_step"), sc.sem("ln_done"), sc.sem("dve_done")
        with nc.Block() as block:
            @block.scalar
            def _(act):
                steps = Steps(act, own)
                for h in range(2):
                    for b in range(B):
                        p, t = pre[:, h, b * S:(b + 1) * S], tmp[:, b * S:(b + 1) * S]
                        if h:
                            wait(act, dve_done, b + 1)
                        steps(act.activation(t, p, ACT.Abs))
                        steps(act.activation(t, t, ACT.Exp, scale=-1.0))
                        act.activation(t, t, ACT.Ln, bias=1.0).then_inc(ln_done, 1)

            @block.vector
            def _(dve):
                for h in range(2):
                    for b in range(B):
                        wait(dve, ln_done, h * B + b + 1)
                        p, t = pre[:, h, b * S:(b + 1) * S], tmp[:, b * S:(b + 1) * S]
                        dve.scalar_tensor_tensor(out=p, in0=p, scalar=0.0, in1=t, op0=ALU.max, op1=ALU.add).then_inc(dve_done, 1)


def selective_scan(nc, dt, xs, zs, bc, bc_sel, A, D_skip, ident):
    NSEG = S // SEG
    with Scope(nc, "scan") as sc:
        dA, dBx = sc.sb("dA", [128, 2, SEG]), sc.sb("dBx", [128, 2, SEG])
        h, hC = sc.sb("h", [128, 2, SEG]), sc.sb("hC", [128, 2, SEG])
        dtx, carry = sc.sb("dtx", [128, 2, SEG]), sc.sb("carry", [128, 2 * D_STATE])
        b_ps, c_ps = sc.ps("b_ps", [128, SEG]), sc.ps("c_ps", [128, SEG])
        y_ps = sc.ps("y_ps", [128, 2, SEG])
        b_ready, c_ready, b_used = sc.sem("b_ready"), sc.sem("c_ready"), sc.sem("b_used")
        decay_ready, scanned, carried = sc.sem("decay_ready"), sc.sem("scanned"), sc.sem("carried")
        hc_ready, hc_used = sc.sem("hc_ready"), sc.sem("hc_used")
        dtx_done, y_taken, gated = sc.sem("dtx_done"), sc.sem("y_taken"), sc.sem("gated")

        alone = sc.sem("dve_waits")

        def u(g, n, k=0):
            return (g * D_STATE + n) * 2 + k

        with nc.Block() as block:
            @block.tensor
            def _(pe):
                def spread(g, n, ps, row, ready):
                    for q in range(SEG // CH):
                        mm = pe.matmul(ps[:, q * CH:(q + 1) * CH], bc_sel[:, bass.ds(n * 128 + row * 128, 128)],
                                       bc[:, bass.ds(g * SEG + q * CH, CH)], start=True, stop=True)
                    mm.then_inc(ready, 1)

                def spread_b(g, n):
                    wait(pe, b_used, u(g, n) + 1)
                    spread(g, n, b_ps, 0, b_ready)

                def spread_c(g, n):
                    wait(pe, hc_ready, u(g, n) + 2)
                    spread(g, n, c_ps, D_STATE, c_ready)

                def add_up(g, n, first, last):
                    for k in range(2):
                        wait(pe, hc_ready, u(g, n, k) + 3)
                        if first:
                            wait(pe, y_taken, g * 2 + (k + 1))
                        for q in range(SEG // CH):
                            mm = pe.matmul(y_ps[:, k, q * CH:(q + 1) * CH], ident, hC[:, k, q * CH:(q + 1) * CH],
                                           start=first, stop=last)
                        mm.then_inc(hc_used, 1)

                with pe.Fori(0, B * NSEG) as g:
                    spread_b(g, 0)
                    spread_c(g, 0)
                    spread_b(g, 1)
                    add_up(g, 0, True, False)
                    spread_c(g, 1)
                    with pe.Fori(1, D_STATE - 1) as n:
                        spread_b(g, n + 1)
                        add_up(g, n, False, False)
                        spread_c(g, n + 1)
                    add_up(g, D_STATE - 1, False, True)

            @block.scalar
            def _(act):
                with act.Fori(0, B * NSEG) as g:
                    with act.Fori(0, D_STATE) as n:
                        for k in range(2):
                            wait(act, scanned, u(g, n, k) + 1)
                            act.activation(dA[:, k, :], dt[:, k, bass.ds(g * SEG, SEG)], ACT.Exp,
                                           scale=A[:, bass.ds(n + k * D_STATE, 1)]).then_inc(decay_ready, 1)

            @block.vector
            def _(dve):
                dve.sem_inc(b_used, 1)
                for credit in (scanned, hc_ready, hc_used, y_taken):
                    dve.sem_inc(credit, 2)

                def segment(g, fresh):
                    now = bass.ds(g * SEG, SEG)
                    for k in range(2):
                        dve.tensor_tensor(dtx[:, k, :], dt[:, k, now], xs[:, k, now], ALU.mult).then_inc(dtx_done, 1)
                    wait(dve, dtx_done, g * 2 + 2, alone)
                    with dve.Fori(0, D_STATE) as n:
                        for k in range(2):
                            if k == 0:
                                wait(dve, b_ready, g * D_STATE + n + 1)
                            dve.tensor_tensor(dBx[:, k, :], dtx[:, k, :], b_ps[:, :], ALU.mult).then_inc(b_used, 1)
                            wait(dve, b_used, u(g, n, k) + 2)
                            wait(dve, decay_ready, u(g, n, k) + 1)
                            wait(dve, hc_ready, u(g, n, k) + 1)
                            state = carry[:, bass.ds(n + k * D_STATE, 1)]
                            dve.tensor_tensor_scan(h[:, k, :], dA[:, k, :], dBx[:, k, :], 0.0 if fresh else state,
                                                   ALU.mult, ALU.add).then_inc(scanned, 1)
                            wait(dve, scanned, u(g, n, k) + 3, alone)
                            dve.tensor_copy(state, h[:, k, SEG - 1:SEG]).then_inc(carried, 1)
                            if k == 0:
                                wait(dve, c_ready, g * D_STATE + n + 1)
                            wait(dve, hc_used, u(g, n, k) + 1)
                            dve.tensor_tensor(hC[:, k, :], h[:, k, :], c_ps[:, :], ALU.mult).then_inc(hc_ready, 1)
                            wait(dve, carried, u(g, n, k) + 1)
                    for k in range(2):
                        wait(dve, hc_used, u(g, D_STATE - 1, k) + 3)
                        dve.scalar_tensor_tensor(out=xs[:, k, now], in0=xs[:, k, now], scalar=D_skip[:, k:k + 1],
                                                 in1=y_ps[:, k, :], op0=ALU.mult, op1=ALU.add).then_inc(y_taken, 1)
                        wait(dve, y_taken, g * 2 + (k + 3))
                        dve.tensor_tensor(xs[:, k, now], xs[:, k, now], zs[:, k, now], ALU.mult).then_inc(gated, 1)

                with dve.Fori(0, B) as b:
                    for s in range(NSEG):
                        segment(b * NSEG + s, s == 0)


def small(nc, name, ops):
    with Scope(nc, name) as sc:
        done = sc.sem("done")
        with nc.Block() as block:
            def run(which):
                def program(eng):
                    for i, (who, make) in enumerate(ops):
                        if who == which:
                            if i:
                                eng.wait_ge(done, i)
                            make(eng).then_inc(done, 1)
                return program
            block.scalar(run("act"))
            block.vector(run("dve"))
            block.tensor(run("pe"))


def build(nc, io):
    Scope.ended = []
    with ExitStack() as top:
        def keep(name, shape, dt=F32):
            return top.enter_context(nc.sbuf_tensor(name, shape, dt))
        x, acc = keep("x", [128, T]), None
        xn = keep("xn", [128, T])
        ct = keep("consts", [128, PACKS["c"].n])
        ident_b = keep("ident_b", [128, 128], BF16)
        C = {k: PACKS["c"].view(ct, k) for k in PACKS["c"].at}
        load(nc, "load_x", [(ct[:, :], io["pack_c"]), (x[:, :], io["x"]), (ident_b[:, :], io["ident_b"])])

        norm(nc, "ln0", x, xn, C["ones"], C["eps5"])
        mamba(nc, x, xn, C, io)
        moe(nc, x, xn, C, ident_b[:, :], io)
        p = PACKS["l1"]
        with Scope(nc, "l1") as sc:
            wt, sel = sc.sb("wt", [128, p.n]), sc.sb("sel", [12, 4 * 128], BF16)
            W = {k: p.view(wt, k) for k in p.at}
            W["ones_row"] = W["ones_row"][0:1, :]
            load(nc, "load_l1", [(wt[:, :], io["pack_l1"]), (sel[:, :], io["sel1"])])
            norm(nc, "ln1", x, xn, C["ones"], C["eps5"])
            linear_attention(nc, x, xn, C, W)
            four_experts(nc, x, xn, C, W, sel, ident_b[:, :])
        p = PACKS["l2"]
        with Scope(nc, "l2w") as sc:
            wt, mt = sc.sb("wt", [128, p.n]), sc.sb("masks", [128, 4 * 128], BF16)
            ones3 = sc.sb("ones3", [3, 128], BF16)
            W = {k: p.view(wt, k) for k in p.at}
            load(nc, "load_l2", [(wt[:, :], io["pack_l2"]), (mt[:, :], io["masks"]), (ones3[:, :], io["ones_b"][:, 0:128])])
            C["ones_b"] = ones3[:, :]
            masks = {k: mt[:, j * 128:(j + 1) * 128] for j, k in enumerate(("neg_qk", "neg_kq", "big_qk", "big_kq"))}
            masks["seen"] = W["seen"]
            small(nc, "roots", [("dve", lambda e: e.reciprocal(W["hyp_c"], W["hyp_c"])),
                                ("act", lambda e: e.activation(W["hyp_root"], W["hyp_c"], ACT.Sqrt))])
            norm(nc, "ln2", x, xn, C["ones"], C["eps5"])
            causal_attention(nc, x, xn, C, W, io, ident_b[:, :], masks)
        p = PACKS["l3"]
        with Scope(nc, "l3w") as sc:
            wt = sc.sb("wt", [128, p.n])
            W = {k: p.view(wt, k) for k in p.at}
            load(nc, "load_l3", [(wt[:, :], io["pack_l3"])])
            norm(nc, "ln3", x, xn, C["ones"], C["eps5"])
            embed_attention(nc, x, xn, C, W, io)
            acc = sc.sb("acc", [128, NT, D])
            routed_attention(nc, x, xn, C, W, acc)
            store(nc, [(io["out"].rearrange("(t p) d -> p t d", p=128), acc[:, :, :])])



def router_logits(pe, ps, src, w, n, biases=None, ones=None):
    for t in range(NT):
        out = ps[:, t * n:(t + 1) * n]
        last = not biases
        mm = pe.matmul(out, src[:, t * 128:(t + 1) * 128], w, start=True, stop=last)
        for k, b in enumerate(biases or []):
            mm = pe.matmul(out, ones, b, start=False, stop=(k == len(biases) - 1))
    return mm


def top_mask(dve, steps, score, sel, k, e, tri, gt, eq, rank):
    other = score.unsqueeze(2).to_broadcast([128, NT, e, e])
    mine = score.unsqueeze(3).to_broadcast([128, NT, e, e])
    front = tri.rearrange("p (a b) -> p a b", a=e).unsqueeze(1).to_broadcast([128, NT, e, e])
    steps(dve.tensor_tensor(gt, other, mine, ALU.is_gt))
    steps(dve.tensor_tensor(eq, other, mine, ALU.is_equal))
    steps(dve.tensor_tensor(eq, eq, front, ALU.mult))
    steps(dve.tensor_tensor(gt, gt, eq, ALU.add))
    steps(dve.tensor_reduce(rank, gt, AX.X, ALU.add))
    steps(dve.tensor_scalar(sel, rank, float(k) - 0.5, None, ALU.is_lt))


def spread_weights(nc, name, w, e, wT, ident_b):
    with Scope(nc, name) as sc:
        parts = sc.sb("parts", [128, NT, 3 * e], BF16)
        rest = sc.sb("rest", [128, NT, e])
        ps = sc.ps("ps", [128, T], BF16)
        own, parts_done, turned, copied = sc.sem("dve_step"), sc.sem("parts_done"), sc.sem("turned"), sc.sem("copied")
        per = 8
        with nc.Block() as block:
            @block.vector
            def _(dve):
                steps = Steps(dve, own)
                hi, mid, low = (parts[:, :, q * e:(q + 1) * e] for q in range(3))
                steps(dve.tensor_copy(hi, w))
                steps(dve.tensor_tensor(rest[:, :, :], w, hi, ALU.subtract))
                steps(dve.tensor_copy(mid, rest[:, :, :]))
                dve.tensor_tensor(low, rest[:, :, :], mid, ALU.subtract).then_inc(parts_done, 1)
                for q in range(NT // per):
                    dve.wait_ge(turned, q + 1)
                    dve.tensor_copy(wT[:, q * per * 128:(q + 1) * per * 128],
                                    ps[0:3 * e, q * per * 128:(q + 1) * per * 128]).then_inc(copied, 1)

            @block.tensor
            def _(pe):
                pe.wait_ge(parts_done, 1)
                for q in range(NT // per):
                    for t in range(q * per, (q + 1) * per):
                        mm = pe.transpose(ps[0:3 * e, t * 128:(t + 1) * 128], parts[:, t, :], ident_b)
                    mm.then_inc(turned, 1)


def route_groups(nc, src, router, tri, w):
    groups, kept, k = 8, 4, 8
    with Scope(nc, "route0") as sc:
        score, work = sc.sb("score", [128, NT, NE0]), sc.sb("work", [128, NT, NE0])
        gsum, gsel, rank = (sc.sb(n, [128, NT, groups]) for n in ("gsum", "gsel", "rank"))
        gt, eq = (sc.sb(n, [128, NT, groups, groups]) for n in ("gt", "eq"))
        top8, total = sc.sb("top8", [128, NT, 8]), sc.sb("total", [128, NT, 1])
        ps = sc.ps("ps", [128, NT * NE0])
        own, logits_ready, scored = sc.sem("dve_step"), sc.sem("logits_ready"), sc.sem("scored")
        maxed = sc.sem("maxed")
        with nc.Block() as block:
            @block.tensor
            def _(pe):
                router_logits(pe, ps, src, router, NE0).then_inc(logits_ready, 1)

            @block.scalar
            def _(act):
                act.wait_ge(logits_ready, 1)
                act.activation(score[:, :, :].rearrange("p t e -> p (t e)"), ps[:, :], ACT.Sigmoid).then_inc(scored, 1)

            @block.vector
            def _(dve):
                steps = Steps(dve, own)
                dve.wait_ge(scored, 1)
                steps(dve.tensor_reduce(gsum[:, :, :], score[:, :, :].rearrange("p t (g k) -> p t g k", g=groups), AX.X, ALU.add))
                top_mask(dve, steps, gsum[:, :, :], gsel[:, :, :], kept, groups, tri, gt[:, :, :, :], eq[:, :, :, :], rank[:, :, :])
                in_group = gsel[:, :, :].unsqueeze(3).to_broadcast([128, NT, groups, NE0 // groups])
                by_group = score[:, :, :].rearrange("p t (g k) -> p t g k", g=groups)
                steps(dve.tensor_tensor(by_group, by_group, in_group, ALU.mult))
                for t in range(NT):
                    ins = dve.max(top8[:, t, :], score[:, t, :])
                steps(ins)
                for t in range(NT):
                    ins = dve.match_replace(work[:, t, :], top8[:, t, :], score[:, t, :], -1.0)
                steps(ins)
                steps(dve.tensor_tensor(work[:, :, :], work[:, :, :], score[:, :, :], ALU.not_equal))
                steps(dve.tensor_tensor(w, score[:, :, :], work[:, :, :], ALU.mult))
                steps(dve.tensor_reduce(total[:, :, 0], w, AX.X, ALU.add))
                steps(dve.tensor_scalar(total[:, :, :], total[:, :, :], 1e-12, None, ALU.max))
                steps(dve.reciprocal(total[:, :, :], total[:, :, :]))
                dve.tensor_tensor(w, w, total[:, :, :].to_broadcast([128, NT, NE0]), ALU.mult).then_inc(maxed, 1)


def moe(nc, x, xn, C, ident_b, io):
    p = PACKS["e"]
    with Scope(nc, "moe") as sc:
        wt, sel = sc.sb("wt", [128, p.n]), sc.sb("sel", [96, 16 * 128], BF16)
        W = {k: p.view(wt, k) for k in p.at}
        w, wT = sc.sb("w", [128, NT, NE0]), sc.sb("wT", [96, T], BF16)
        load(nc, "load_e", [(wt[:, :], io["pack_e"]), (sel[:, :], io["moe_sel"])])
        route_groups(nc, xn, W["router"], C["tri8"], w[:, :, :])
        spread_weights(nc, "spread0", w[:, :, :], NE0, wT, ident_b)
        blk = slice(0, 128)
        expert_blocks(nc, "experts", xn, [
            dict(gate=W["gate"][:, j * 128:(j + 1) * 128], up=W["up"][:, j * 128:(j + 1) * 128], func=ACT.Silu,
                 down=W["down"][:, j * 128:(j + 1) * 128], sel=sel[:, j * 128:(j + 1) * 128]) for j in range(16)] + [
            dict(gate=W["sgate"], up=W["sup"], func=ACT.Silu, down=W["sdown"])], wT, x, x)



NE1 = 4


def cumulative_attention(nc, x, e, keys, values, one):
    with Scope(nc, "cumulative") as sc:
        sums = sc.sb("sums", [128, T])
        own, weighted = sc.sem("dve_step"), sc.sem("weighted")
        with nc.Block() as block:
            @block.vector
            def _(dve):
                steps = Steps(dve, own)
                ones = one.to_broadcast([128, S])
                for b in range(B):
                    at = slice(b * S, (b + 1) * S)
                    steps(dve.tensor_tensor_scan(sums[:, at], ones, e[:, at], 0.0, ALU.mult, ALU.add))
                    steps(dve.reciprocal(sums[:, at], sums[:, at]))
                    steps(dve.tensor_tensor(e[:, at], e[:, at], sums[:, at], ALU.mult))
                    steps(dve.tensor_tensor(e[:, at], e[:, at], keys[:, at], ALU.mult))
                    steps(dve.tensor_tensor_scan(sums[:, at], ones, e[:, at], 0.0, ALU.mult, ALU.add))
                    steps(dve.tensor_tensor(sums[:, at], sums[:, at], values[:, at], ALU.mult))
                    dve.tensor_tensor(x[:, at], x[:, at], sums[:, at], ALU.add).then_inc(weighted, 1)


def route_softmax(nc, src, router, biases, ones_row, tri, w):
    with Scope(nc, "route1") as sc:
        logit, sel, rank, ex = (sc.sb(n, [128, NT, NE1]) for n in ("logit", "sel", "rank", "ex"))
        gt, eq = (sc.sb(n, [128, NT, NE1, NE1]) for n in ("gt", "eq"))
        top, total = sc.sb("top", [128, NT, 1]), sc.sb("total", [128, NT, 1])
        ps = sc.ps("ps", [128, NT * NE1])
        own, logits_ready, shifted, exped = sc.sem("dve_step"), sc.sem("logits_ready"), sc.sem("shifted"), sc.sem("exped")
        with nc.Block() as block:
            @block.tensor
            def _(pe):
                router_logits(pe, ps, src, router, NE1, biases, ones_row).then_inc(logits_ready, 1)

            @block.scalar
            def _(act):
                act.wait_ge(shifted, 1)
                act.activation(ex[:, :, :], rank[:, :, :], ACT.Exp).then_inc(exped, 1)

            @block.vector
            def _(dve):
                steps = Steps(dve, own)
                dve.wait_ge(logits_ready, 1)
                steps(dve.tensor_copy(logit[:, :, :].rearrange("p t e -> p (t e)"), ps[:, :]))
                top_mask(dve, steps, logit[:, :, :], sel[:, :, :], 2, NE1, tri, gt[:, :, :, :], eq[:, :, :, :], rank[:, :, :])
                steps(dve.tensor_reduce(top[:, :, 0], logit[:, :, :], AX.X, ALU.max))
                dve.tensor_tensor(rank[:, :, :], logit[:, :, :], top[:, :, :].to_broadcast([128, NT, NE1]),
                                  ALU.subtract).then_inc(shifted, 1)
                dve.wait_ge(exped, 1)
                steps(dve.tensor_tensor(w, ex[:, :, :], sel[:, :, :], ALU.mult))
                steps(dve.tensor_reduce(total[:, :, 0], w, AX.X, ALU.add))
                steps(dve.reciprocal(total[:, :, :], total[:, :, :]))
                steps(dve.tensor_tensor(w, w, total[:, :, :].to_broadcast([128, NT, NE1]), ALU.mult))


def weighted_sum(nc, name, x, consts, product, wT):
    n = len(consts) + 1
    with Scope(nc, name) as sc:
        w_ps, o_ps = sc.ps("w_ps", [128, n, CH]), sc.ps("o_ps", [128, CH])
        o_sb = sc.sb("o_sb", [128, CH])
        spread, out_ready, out_copied = sc.sem("spread"), sc.sem("out_ready"), sc.sem("out_copied")
        own, done = sc.sem("dve_step"), sc.sem("done")
        sel, lhsT, src, bias = product
        with nc.Block() as block:
            @block.tensor
            def _(pe):
                with pe.Fori(0, NC) as c:
                    wait(pe, done, c + 1)
                    for k, s in enumerate([s for s, _ in consts] + [sel]):
                        mm = pe.matmul(w_ps[:, k, :], s, cols(wT, c), start=True, stop=True)
                    mm.then_inc(spread, 1)
                    pe.matmul(o_ps[:, :], lhsT, cols(src, c), start=True, stop=True).then_inc(out_ready, 1)

            @block.scalar
            def _(act):
                with act.Fori(0, NC) as c:
                    wait(act, out_ready, c + 1)
                    act.activation(o_sb[:, :], o_ps[:, :], ACT.Identity, bias=bias).then_inc(out_copied, 1)

            @block.vector
            def _(dve):
                dve.sem_inc(done, 1)
                steps = Steps(dve, own)
                with steps.loop(NC, n) as c:
                    wait(dve, spread, c + 1)
                    for k, (_, b) in enumerate(consts):
                        steps(dve.scalar_tensor_tensor(out=cols(x, c), in0=w_ps[:, k, :], scalar=b, in1=cols(x, c),
                                                       op0=ALU.mult, op1=ALU.add))
                    wait(dve, out_copied, c + 1)
                    steps(dve.tensor_tensor(o_sb[:, :], o_sb[:, :], w_ps[:, n - 1, :], ALU.mult))
                    dve.tensor_tensor(cols(x, c), cols(x, c), o_sb[:, :], ALU.add).then_inc(done, 1)


def linear_attention(nc, x, xn, C, W):
    with Scope(nc, "l1a") as sc:
        h, keys, values, e = (sc.sb(n, [128, T]) for n in ("h", "keys", "values", "e"))
        norm(nc, "ln_attn", xn, h, C["ones"], C["eps5"], gain=W["gamma"], shift=W["beta"])
        root = float(np.float32(1.0 / np.sqrt(D)))
        small(nc, "bka", [("dve", lambda d: d.tensor_scalar(W["bka"], W["bka"], root, None, ALU.mult))])
        linear(nc, "kv", [dict(terms=[(W["Wk"], h)], dst=keys, by="act", bias=W["bk"]),
                          dict(terms=[(W["Wv"], h)], dst=values, by="act", bias=W["bv"]),
                          dict(terms=[(W["Wka"], keys)], dst=e, by="act", bias=W["bka"], scale=root, func=ACT.Exp, after=0)])
        cumulative_attention(nc, x, e, keys, values, C["one"])


def fold_weights(nc, W):
    with Scope(nc, "fold") as sc:
        ps = sc.ps("ps", [128, 8, CH])
        t = sc.sb("t", [128, 2, 128])
        v = sc.sb("v", [128, 2])

        def mm(k, lhsT, rhs):
            n = rhs.shape[1]
            return ("pe", lambda e: e.matmul(ps[:, k, 0:n], lhsT, rhs, start=True, stop=True))

        def copy(dst, k):
            return ("dve", lambda e: e.tensor_copy(dst, ps[:, k, 0:dst.shape[1]]))

        def plus(dst, k, other):
            return ("dve", lambda e: e.tensor_tensor(dst, ps[:, k, 0:dst.shape[1]], other, ALU.add))

        small(nc, "fold_ops", [
            mm(0, W["ce_wv"], W["ce_synT"]), copy(t[:, 0, :], 0),
            mm(1, t[:, 0, :], W["ce_wo"]), plus(W["ce_syn"], 1, W["ce_syn"]),
            mm(2, W["ce_wv"], W["ce_synb"]), plus(v[:, 0:1], 2, W["ce_bv"]),
            mm(3, W["ce_wo"], v[:, 0:1]), plus(v[:, 1:2], 3, W["ce_bo"]),
            ("dve", lambda e: e.tensor_tensor(W["ce_synb"], W["ce_synb"], v[:, 1:2], ALU.add)),
            mm(4, W["me_wv"], W["me_eqT"]), copy(t[:, 1, :], 4),
            mm(5, W["me_wo"], t[:, 1, :]), copy(t[:, 0, :], 5),
            mm(6, W["me_wv"], W["me_eqb"]), plus(v[:, 0:1], 6, W["me_bv"]),
            mm(7, W["me_wo"], v[:, 0:1]), plus(v[:, 1:2], 7, W["me_bo"]),
            mm(0, W["me_c1"][:, 0:128], v[:, 1:2]), mm(1, W["me_c1"][:, 128:256], v[:, 1:2]),
            plus(W["me_c1b"][:, 0:1], 0, W["me_c1b"][:, 0:1]), plus(W["me_c1b"][:, 1:2], 1, W["me_c1b"][:, 1:2]),
            mm(2, t[:, 0, :], W["me_c1"]), copy(W["me_c1"], 2)])


def four_experts(nc, x, xn, C, W, sel, ident_b):
    with Scope(nc, "l1f") as sc:
        w, wT = sc.sb("w", [128, NT, NE1]), sc.sb("wT", [3 * NE1, T], BF16)
        pick = [sel[:, e * 128:(e + 1) * 128] for e in range(NE1)]
        route_softmax(nc, xn, W["router"], [W["router_b"], W["balancer"]], W["ones_row"], C["tri4"], w[:, :, :])
        spread_weights(nc, "spread1", w[:, :, :], NE1, wT, ident_b)
        fold_weights(nc, W)

        def part(name, j):
            return W[name][:, j * 128:(j + 1) * 128]

        expert_blocks(nc, "e013", xn, [
            dict(gate=part("sw1", j), up=part("sw3", j), func=ACT.Silu, down=part("sw2", j), sel=pick[0]) for j in range(4)] + [
            dict(gate=part("me_c1", j), bias=W["me_c1b"][:, j:j + 1], func=ACT.Gelu, down=part("me_c2", j), sel=pick[1])
            for j in range(2)] + [
            dict(gate=part("ml1", j), bias=W["ml_b1"][:, j:j + 1], func=ACT.Gelu, down=part("ml2", j), sel=pick[3])
            for j in range(4)], wT, x, x)
        s, h2, r = sc.sb("s", [128, T]), sc.sb("h2", [128, T]), sc.sb("r", [128, 2, T])
        linear(nc, "syn", [dict(terms=[(W["ce_syn"], xn)], dst=s, by="act", bias=W["ce_synb"])])
        norm(nc, "ln_n1", s, h2, C["ones"], C["eps5"], gain=W["n1g"], shift=W["n1b"])
        linear(nc, "f1", [dict(terms=[(part("f1", j), h2)], dst=r[:, j, :], by="act", func=ACT.Relu, bias=W["f1b"][:, j:j + 1])
                          for j in range(2)])
        linear(nc, "f2", [dict(terms=[(part("f2", j), r[:, j, :]) for j in range(2)], dst=s, by="dve", bias=W["f2b"], add=h2)])
        norm(nc, "ln_n2", s, h2, C["ones"], C["eps5"], gain=W["n2g"], shift=W["n2b"])
        weighted_sum(nc, "gen", x, [(pick[1], W["me_c2b"]), (pick[3], W["ml_b2"])], (pick[2], W["gen"], h2, W["gen_b"]), wT)



HEADS, HD = 16, 8
N_DOT, N_HYP = 6, 4
ST = S // 128
BIG = 1e9


def rotate(nc, name, a, swapped, cos, sin):
    with Scope(nc, name) as sc:
        own = sc.sem("dve_step")
        with nc.Block() as block:
            @block.vector
            def _(dve):
                steps = Steps(dve, own)
                for b in range(B):
                    at = slice(b * S, (b + 1) * S)
                    steps(dve.tensor_tensor(swapped[:, at], swapped[:, at], sin, ALU.mult))
                    steps(dve.tensor_tensor(a[:, at], a[:, at], cos, ALU.mult))
                    steps(dve.tensor_tensor(a[:, at], a[:, at], swapped[:, at], ALU.add))


def token_major(nc, name, src, w, n, dst):
    per = CH // n
    with Scope(nc, name) as sc:
        ps = sc.ps("ps", [128, NT * n])
        made, copied = sc.sem("made"), sc.sem("copied")
        with nc.Block() as block:
            @block.tensor
            def _(pe):
                for t in range(NT):
                    mm = pe.matmul(ps[:, t * n:(t + 1) * n], src[:, t * 128:(t + 1) * 128], w, start=True, stop=True)
                    if t % per == per - 1:
                        mm.then_inc(made, 1)

            @block.scalar
            def _(act):
                for q in range(NT // per):
                    act.wait_ge(made, q + 1)
                    act.activation(dst[:, q * per:(q + 1) * per, :],
                                   ps[:, q * CH:(q + 1) * CH].rearrange("p (t n) -> p t n", n=n), ACT.Copy).then_inc(copied, 1)


def head_factors(nc, name, a, blocks8, base, cosine, time, inv_c, c_col):
    with Scope(nc, name) as sc:
        ps = sc.ps("ps", [128, NC * CH])
        n2, f = sc.sb("n2", [128, T]), sc.sb("f", [128, T])
        squared, summed, copied, rooted, own = (sc.sem(n) for n in ("squared", "summed", "copied", "rooted", "dve_step"))
        timed = sc.sem("timed")
        with nc.Block() as block:
            @block.tensor
            def _(pe):
                with pe.Fori(0, NC) as c:
                    wait(pe, squared, c + 1)
                    pe.matmul(cols(ps, c), blocks8, cols(n2, c), start=True, stop=True).then_inc(summed, 1)

            @block.scalar
            def _(act):
                with act.Fori(0, NC) as c:
                    act.activation(cols(n2, c), cols(a, c), ACT.Square).then_inc(squared, 1)
                act.wait_ge(summed, NC)
                act.activation(time[:, :], ps[:, :], ACT.Sqrt, bias=inv_c).then_inc(timed, 1)
                act.wait_ge(copied, 1)
                act.activation(f[:, :], f[:, :], ACT.Sqrt).then_inc(rooted, 1)

            @block.vector
            def _(dve):
                steps = Steps(dve, own)
                dve.wait_ge(timed, 1)
                dve.tensor_scalar(f[:, :], ps[:, :], 1e-24, None, ALU.max).then_inc(copied, 1)
                if c_col is not None:
                    steps(dve.tensor_scalar(time[:, :], time[:, :], c_col, None, ALU.mult))
                dve.wait_ge(rooted, 1)
                steps(dve.reciprocal(f[:, :], f[:, :]))
                steps(dve.tensor_scalar(f[:, :], f[:, :], cosine, base, ALU.mult, ALU.add))
                steps(dve.tensor_tensor(a[:, :], a[:, :], f[:, :], ALU.mult))


def store_parts(nc, name, src, rows, dests):
    width = src.shape[1]
    with Scope(nc, name) as sc:
        parts, rest = sc.sb("parts", [128, 3, width], BF16), sc.sb("rest", [128, width])
        own, split, stored = sc.sem("dve_step"), sc.sem("split"), sc.sem("stored")
        with nc.Block() as block:
            @block.vector
            def _(dve):
                steps = Steps(dve, own)
                steps(dve.tensor_copy(parts[:, 0, :], src))
                steps(dve.tensor_tensor(rest[:, :], src, parts[:, 0, :], ALU.subtract))
                steps(dve.tensor_copy(parts[:, 1, :], rest[:, :]))
                dve.tensor_tensor(parts[:, 2, :], rest[:, :], parts[:, 1, :], ALU.subtract).then_inc(split, 1)

            @block.sync
            def _(sp):
                sp.wait_ge(split, 1)
                for q, dram in dests:
                    sp.dma_start(dram, parts[rows, q, :]).then_inc(stored, 16)
                sp.wait_ge(stored, 16 * len(dests))


def store_rows(nc, name, m, n, dram, ident_b, negate):
    with Scope(nc, name) as sc:
        parts, rest = sc.sb("parts", [128, 3, n], BF16), sc.sb("rest", [128, n])
        turned_sb = sc.sb("turned", [128, 3, 2, 128], BF16)
        ps = sc.ps("ps", [128, 3, 2, 128], BF16)
        own, split, turned, copied, stored = (sc.sem(k) for k in ("dve_step", "split", "turned_", "copied", "stored"))
        pieces = [(o, min(128, n - o)) for o in range(0, n, 128)]
        with nc.Block() as block:
            @block.vector
            def _(dve):
                steps = Steps(dve, own)
                if negate:
                    steps(dve.tensor_scalar(m, m, -1.0, None, ALU.mult))
                steps(dve.tensor_copy(parts[:, 0, :], m))
                steps(dve.tensor_tensor(rest[:, :], m, parts[:, 0, :], ALU.subtract))
                steps(dve.tensor_copy(parts[:, 1, :], rest[:, :]))
                dve.tensor_tensor(parts[:, 2, :], rest[:, :], parts[:, 1, :], ALU.subtract).then_inc(split, 1)
                dve.wait_ge(turned, 3)
                for k, (o, w) in enumerate(pieces):
                    dve.tensor_copy(turned_sb[0:w, :, k, :], ps[0:w, :, k, :]).then_inc(copied, 1)

            @block.tensor
            def _(pe):
                pe.wait_ge(split, 1)
                for q in range(3):
                    for k, (o, w) in enumerate(pieces):
                        mm = pe.transpose(ps[0:w, q, k, :], parts[:, q, o:o + w], ident_b)
                    mm.then_inc(turned, 1)

            @block.sync
            def _(sp):
                sp.wait_ge(copied, len(pieces))
                for q in range(3):
                    for k, (o, w) in enumerate(pieces):
                        sp.dma_start(dram[q, o:o + w, :], turned_sb[0:w, q, k, :]).then_inc(stored, 16)
                sp.wait_ge(stored, 48 * len(pieces))


Q_STACK, K_STACK = (0, 0, 0, 1, 1, 2), (0, 1, 2, 0, 1, 0)
NP = len(Q_STACK)


def load_stacks(sp, q_dst, k_dst, qd, kd, head, b, sem, rows=HD, at=0):
    tok = bass.ds(b * S, S)
    for dst, src in ((q_dst, qd), (k_dst, kd)):
        stack = src[bass.ds(head, 1), :, :, tok].rearrange("h s d t -> (h s d) t")
        sp.dma_start(dst[at:at + NP * rows, :], stack).then_inc(sem, 16)
    return 2


def row_extremes(nc, name, loads, rows, heads, m, op, mask, ident_b, causal=True):
    with Scope(nc, name) as sc:
        q, k = sc.sb("q", [rows, 2, S], BF16), sc.sb("k", [rows, 2, S], BF16)
        mt = sc.sb("mt", [128, 2, ST])
        ps = sc.ps("ps", [128, 2, S])
        loaded = [sc.sem("loaded0"), sc.sem("loaded1")]
        scored, reduced, kept, alone = sc.sem("scored"), sc.sem("reduced"), sc.sem("kept"), sc.sem("dve_waits")
        n_dma = [0]
        pairs = heads // 2
        with nc.Block() as block:
            @block.sync
            def _(sp):
                with sp.Fori(0, B) as b:
                    with sp.Fori(0, pairs) as hp:
                        for p in range(2):
                            sp.wait_ge(scored, ((b * pairs + hp) * 2 + (p + 1 - 2)) * ST + 2 * ST)
                            n_dma[0] = loads(sp, q[:, p, :], k[:, p, :], hp * 2 + p, b, loaded[p])

            @block.tensor
            def _(pe):
                pe.sem_inc(scored, 2 * ST)
                with pe.Fori(0, B * pairs) as hp:
                    for p in range(2):
                        pe.wait_ge(loaded[p], (hp + 1) * (16 * n_dma[0]))
                        for i in range(ST):
                            pe.wait_ge(reduced, (hp * 2 + p) * ST + (i + 1))
                            n = (i + 1) * 128 if causal else S
                            for o in range(0, n, CH):
                                w = min(CH, n - o)
                                diagonal = causal and o + w == n
                                mm = pe.matmul(ps[:, i % 2, o:o + w], q[:, p, i * 128:(i + 1) * 128], k[:, p, o:o + w],
                                               start=True, stop=not diagonal)
                                if diagonal:
                                    mm = pe.matmul(ps[:, i % 2, n - 128:n], ident_b, mask, start=False, stop=True)
                            mm.then_inc(scored, 1)

            @block.vector
            def _(dve):
                dve.sem_inc(reduced, 2)
                with dve.Fori(0, B * pairs) as hp:
                    for p in range(2):
                        for i in range(ST):
                            dve.wait_ge(scored, (hp * 2 + p) * ST + (i + 1 + 2 * ST))
                            n = (i + 1) * 128 if causal else S
                            dve.tensor_reduce(mt[:, p, i:i + 1], ps[:, i % 2, 0:n], AX.X, op).then_inc(reduced, 1)
                        wait(dve, reduced, (hp * 2 + p) * ST + (ST + 2), alone)
                        dve.tensor_copy(m[:, bass.ds((hp * 2 + p) * ST, ST)], mt[:, p, :]).then_inc(kept, 1)
                        wait(dve, kept, hp * 2 + (p + 1), alone)


STEPS = [(qc, st, 128 * max(st - 4 * qc, 0)) for qc in range(CPB) for st in range(4 * qc + 4)]


def causal_pass(nc, name, loads, rows, pairs, head0, values, o_dram, z_dram, mask_b, ident_b, chain=None):
    nh = 2 * len(STEPS)
    SP_RING, P_RING = 3, 4
    with Scope(nc, name) as sc:
        q, k = sc.sb("q", [rows, 4, S], BF16), sc.sb("k", [rows, 4, S], BF16)
        vq = sc.sb("vq", [128, ST, 4, 32])
        P = sc.sb("P", [128, P_RING, 2, CH])
        o_sb = sc.sb("o_sb", [128, S])
        s_ps, o_ps = sc.ps("s_ps", [128, SP_RING, 2, CH]), sc.ps("o_ps", [128, CH])
        loaded, v_ready = sc.sem("loaded"), sc.sem("v_ready")
        scored, exped, summed = sc.sem("scored"), sc.sem("exped"), sc.sem("summed")
        o_copied, o_stored, pool_step = sc.sem("o_copied"), sc.sem("o_stored"), sc.sem("pool_step")
        alone, sp_waits = sc.sem("pool_waits"), sc.sem("sp_waits")
        n_dma = [0]
        ch = chain(sc, P, s_ps) if chain else None
        with nc.Block() as block:
            @block.sync
            def _(sp):
                with sp.Fori(0, pairs) as hp:
                    sp.wait_ge(summed, (hp + 1) * nh)
                    n_dma[0] = 0
                    for j in range(4):
                        n_dma[0] += loads(sp, q[:, j, :], k[:, j, :], hp * 2 + j % 2, j // 2, loaded)
                    if ch:
                        n_dma[0] += ch["load"](sp, hp, loaded)
                    wait(sp, o_copied, hp * CPB + (CPB + 1), sp_waits)
                    for j in range(4):
                        head = hp * 2 + (j % 2 + head0)
                        tok = slice((j // 2) * S, (j // 2 + 1) * S)
                        sp.dma_start(o_dram[bass.ds(head * HD, HD), tok], o_sb[32 * j:32 * j + HD, :]).then_inc(o_stored, 16)
                        sp.dma_start(z_dram[bass.ds(head * HD, HD), tok], o_sb[32 * j + HD:32 * j + 2 * HD, :]).then_inc(o_stored, 16)
                    wait(sp, o_stored, (hp + 1) * 128, sp_waits)

            @block.gpsimd
            def _(pool):
                pool.memset(vq[:, :, :, :], 1.0).then_inc(pool_step, 1)
                pool.wait_ge(pool_step, 1)
                with pool.Fori(0, pairs) as hp:
                    wait(pool, summed, (hp + 1) * nh, alone)
                    for b in range(B):
                        src = values[:, b * ST:(b + 1) * ST, bass.ds(hp * 2 * HD + head0 * HD, 2 * HD)]
                        pool.tensor_copy(vq[:, :, 2 * b:2 * b + 2, 0:HD], src.rearrange("p t (v d) -> p t v d", v=2)).then_inc(v_ready, 1)

            @block.tensor
            def _(pe):
                pe.sem_inc(summed, nh)

                def score(hp, n):
                    qc, st, lo = STEPS[n // 2]
                    slot = n % SP_RING
                    pe.wait_ge(ch["freed"] if ch else exped, hp * nh + (n + 1 if n >= SP_RING else SP_RING))
                    diagonal = st >= 4 * qc
                    for v in range(2):
                        j = 2 * (n % 2) + v
                        mm = pe.matmul(s_ps[:, slot, v, lo:CH], k[:, j, st * 128:(st + 1) * 128],
                                       q[:, j, qc * CH + lo:(qc + 1) * CH], start=True, stop=not diagonal)
                        if diagonal:
                            mm = pe.matmul(s_ps[:, slot, v, lo:lo + 128], ident_b, mask_b, start=False, stop=True)
                    mm.then_inc(scored, 1)

                def weigh(hp, n):
                    qc, st, lo = STEPS[n // 2]
                    pe.wait_ge(exped, hp * nh + (n + 1 + SP_RING))
                    if st == 0:
                        pe.wait_ge(o_copied, hp * CPB + (qc + 1))
                    for v in range(2):
                        j = 2 * (n % 2) + v
                        mm = pe.matmul(o_ps[32 * j:32 * j + 32, lo:CH], vq[:, st, j, :], P[:, n % P_RING, v, lo:CH],
                                       start=(st == 0), stop=(st == 4 * qc + 3))
                    mm.then_inc(summed, 1)

                with pe.Fori(0, pairs) as hp:
                    pe.wait_ge(loaded, (hp + 1) * (16 * n_dma[0]))
                    pe.wait_ge(v_ready, hp * 2 + 2)
                    if ch:
                        ch["pe"](pe, hp, s_ps)
                    score(hp, 0)
                    score(hp, 1)
                    for n in range(0, nh, 2):
                        if n + 2 < nh:
                            score(hp, n + 2)
                            score(hp, n + 3)
                        weigh(hp, n)
                        weigh(hp, n + 1)

            @block.scalar
            def _(act):
                if ch:
                    ch["act"](act, pairs, nh, scored, exped, summed)
                    return
                act.sem_inc(exped, SP_RING)
                with act.Fori(0, pairs) as hp:
                    for n in range(nh):
                        lo = STEPS[n // 2][2]
                        act.wait_ge(scored, hp * nh + (n + 1))
                        act.wait_ge(summed, hp * nh + (n + 1 - P_RING + nh))
                        act.activation(P[:, n % P_RING, :, lo:CH], s_ps[:, n % SP_RING, :, lo:CH], ACT.Exp).then_inc(exped, 1)

            @block.vector
            def _(dve):
                dve.sem_inc(o_copied, 1)
                with dve.Fori(0, pairs) as hp:
                    def collect(qc):
                        dve.wait_ge(summed, hp * nh + (sum(2 * (4 * c + 4) for c in range(qc + 1)) + nh))
                        if qc == 0:
                            dve.wait_ge(loaded, (hp + 1) * (16 * n_dma[0]))
                        dve.tensor_copy(o_sb[:, qc * CH:(qc + 1) * CH], o_ps[:, :]).then_inc(o_copied, 1)

                    if ch:
                        ch["dve"](dve, hp, nh, scored, exped, collect)
                    else:
                        for qc in range(CPB):
                            collect(qc)


def causal_attention(nc, x, xn, C, W, io, ident_b, masks):
    with Scope(nc, "l2") as sc:
        qd = nc.dram_tensor("q_stack", (HEADS, NP, HD, T), BF16).ap()
        kd = nc.dram_tensor("k_stack", (HEADS, NP, HD, T), BF16).ap()
        qtd = nc.dram_tensor("q_time", (N_HYP, NP, 1, T), BF16).ap()
        ktd = nc.dram_tensor("k_time", (N_HYP, NP, 1, T), BF16).ap()
        m_dot = nc.dram_tensor("m_dot", (3, B * N_DOT * ST, 128), BF16).ap()
        m_hyp = nc.dram_tensor("m_hyp", (3, B * N_HYP * ST, 128), BF16).ap()
        o_dram = nc.dram_tensor("o_sums", (128, T), F32).ap()
        z_dram = nc.dram_tensor("o_weights", (128, T), F32).ap()
        small(nc, "curv", [
            ("dve", lambda e: e.reciprocal(W["inv_c"], W["c"])),
            ("dve", lambda e: e.scalar_tensor_tensor(out=W["q_base"], in0=W["c"], scalar=W["hyp"], in1=W["q_base"],
                                                     op0=ALU.mult, op1=ALU.subtract)),
            ("dve", lambda e: e.tensor_scalar(W["q_base"], W["q_base"], -1.0, None, ALU.mult)),
            ("act", lambda e: e.activation(W["root_inv_c"], W["inv_c"], ACT.Sqrt))])
        with Scope(nc, "l2p") as sp_:
            a, t, time = sp_.sb("a", [128, T]), sp_.sb("t", [128, T]), sp_.sb("time", [128, T])
            cos, sin = sp_.sb("cos", [128, S]), sp_.sb("sin", [128, S])
            load(nc, "load_rot", [(cos[:, :], io["rot_cos"]), (sin[:, :], io["rot_sin"])])
            for n, dram, tdram, stack in (("q", qd, qtd, Q_STACK), ("k", kd, ktd, K_STACK)):
                linear(nc, f"proj_{n}", [dict(terms=[(W["W" + n], xn)], dst=a, by="act"),
                                         dict(terms=[(W["W" + n + "s"], xn)], dst=t, by="dve")])
                rotate(nc, f"rot_{n}", a, t, cos[:, :], sin[:, :])
                head_factors(nc, f"factor_{n}", a, W["blocks8"], W[n + "_base"], W[n + "_cos"], time, W["inv_c"],
                             W["c"] if n == "q" else None)
                store_parts(nc, f"parts_{n}", a[:, :], slice(0, 128),
                            [(part, dram[:, at, :, :]) for at, part in enumerate(stack)])
                store_parts(nc, f"timeparts_{n}", time[:, :], slice(N_DOT * HD, (N_DOT + N_HYP) * HD, HD),
                            [(part, tdram[:, at, 0, :]) for at, part in enumerate(stack)])
        values = sc.sb("values", [128, NT, 128])
        token_major(nc, "proj_v", xn, W["Wv"], 128, values)
        m = sc.sb("m", [128, B * N_DOT * ST])

        def dot_loads(sp, q, k, head, b, sem):
            return load_stacks(sp, q, k, qd, kd, head, b, sem)

        row_extremes(nc, "dot_max", dot_loads, 48, N_DOT, m, ALU.max, masks["neg_qk"], ident_b)
        store_rows(nc, "dot_m", m[:, :], B * N_DOT * ST, m_dot, ident_b, True)
        m_rows = m_dot.rearrange("q (b h i) t -> q b h (i t)", b=B, h=N_DOT)

        def dot_b_loads(sp, q, k, head, b, sem):
            sp.dma_start(q[48:51, :], m_rows[:, b, bass.ds(head, 1), :].rearrange("q h t -> q (h t)")).then_inc(sem, 16)
            sp.dma_start(k[48:51, :], io["ones_b"][0:3, 0:S]).then_inc(sem, 16)
            return load_stacks(sp, q, k, qd, kd, head, b, sem) + 2

        causal_pass(nc, "dot", dot_b_loads, 51, N_DOT // 2, 0, values, o_dram, z_dram, masks["neg_kq"], ident_b)

        def cos_loads(sp, q, k, head, b, sem):
            return load_stacks(sp, q, k, qd, kd, head + (N_DOT + N_HYP), b, sem)

        causal_pass(nc, "cos", cos_loads, 48, (HEADS - N_DOT - N_HYP) // 2, N_DOT + N_HYP, values, o_dram, z_dram,
                    masks["neg_kq"], ident_b)
        hyperbolic(nc, C, W, qd, kd, qtd, ktd, m_hyp, values, o_dram, z_dram, io, ident_b, masks)
        with Scope(nc, "l2o") as so:
            y, z = so.sb("y", [128, T]), so.sb("z", [128, T])
            load(nc, "load_y", [(y[:, :], o_dram), (z[:, :], z_dram)])
            small(nc, "divide", [("dve", lambda e: e.reciprocal(z[:, :], z[:, :])),
                                 ("dve", lambda e: e.tensor_tensor(y[:, :], y[:, :], z[:, :], ALU.mult)),
                                 ("act", lambda e: e.activation(W["bin"], W["bin"], ACT.Sign))])
            linear(nc, "proj_o", [dict(terms=[(W["Wo"], y), (W["bin"], xn)], dst=x, by="dve", bias=W["proj_b"], add=x)])


def hyperbolic(nc, C, W, qd, kd, qtd, ktd, m_hyp, values, o_dram, z_dram, io, ident_b, masks):
    least = float(np.float32(1.0 + 1e-7))
    rows = 54

    def loads(sp, q, k, head, b, sem):
        return (load_stacks(sp, q, k, qd, kd, head + N_DOT, b, sem) +
                load_stacks(sp, q, k, qtd, ktd, head, b, sem, rows=1, at=48))

    with Scope(nc, "hyp") as sc:
        m = sc.sb("m", [128, B * N_HYP * ST])
        t = sc.sb("t", [128, B * N_HYP * ST])
        row_extremes(nc, "hyp_min", loads, rows, N_HYP, m, ALU.min, masks["big_qk"], ident_b)
        per_head = m[:, :].rearrange("p (b h i) -> p h b i", b=B, h=N_HYP)
        small(nc, "hyp_m", [
            ("dve", lambda e: e.tensor_scalar(m[:, :], m[:, :], least, None, ALU.max)),
            ("act", lambda e: e.activation(t[:, :], m[:, :], ACT.Square)),
            ("act", lambda e: e.activation(t[:, :], t[:, :], ACT.Ln, bias=C["minus_one"])),
            ("act", lambda e: e.activation(t[:, :], t[:, :], ACT.Exp, scale=0.5)),
            ("dve", lambda e: e.tensor_tensor(m[:, :], m[:, :], t[:, :], ALU.add)),
            ("act", lambda e: e.activation(m[:, :], m[:, :], ACT.Ln))] + [
            ("dve", lambda e, h=h: e.tensor_scalar(per_head[:, h, :, :], per_head[:, h, :, :], W["hyp_root"][:, h:h + 1], 1e-6,
                                                   ALU.mult, ALU.add)) for h in range(N_HYP)] + [
            ("act", lambda e: e.activation(m[:, :], m[:, :], ACT.Ln)),
            ("act", lambda e: e.activation(m[:, :], m[:, :], ACT.Exp, scale=-1.0))])
        store_rows(nc, "hyp_rows", m[:, :], B * N_HYP * ST, m_hyp, ident_b, False)
        m_rows = m_hyp.rearrange("q (b h i) t -> q b h (i t)", b=B, h=N_HYP)

        def chain(sc2, P, s_ps):
            mr = sc2.sb("mr", [3, 4, S], BF16)
            mb = sc2.sb("mb", [128, CPB, 4, CH])
            a, u = sc2.sb("a", [128, 4, 2, CH]), sc2.sb("u", [128, 4, 2, CH])
            roots = sc2.sb("roots", [128, 2])
            freed, spread, m_done = sc2.sem("freed"), sc2.sem("spread"), sc2.sem("m_done")
            clipped, rooted, added, logged, shifted = (sc2.sem(n) for n in ("clipped", "rooted", "added", "logged", "shifted"))
            own_a, exp_raw = sc2.sem("act_step"), sc2.sem("exp_raw")
            RING = 3

            def load_m(sp, hp, sem):
                for j in range(4):
                    sp.dma_start(mr[:, j, :], m_rows[:, j // 2, bass.ds(hp * 2 + j % 2, 1), :].rearrange("q h t -> q (h t)")).then_inc(sem, 16)
                return 4

            def pe_part(pe, hp, s_ps):
                for qc in range(CPB):
                    for half in range(2):
                        n = qc * 2 + half
                        if n == 0:
                            pe.wait_ge(freed, hp * (2 * len(STEPS)) + RING)
                        if n >= RING:
                            pe.wait_ge(m_done, hp * 8 + (n - RING + 1))
                        for v in range(2):
                            mm = pe.matmul(s_ps[:, n % RING, v, :], C["ones_b"], mr[:, 2 * half + v, qc * CH:(qc + 1) * CH],
                                           start=True, stop=True)
                        mm.then_inc(spread, 1)
                pe.wait_ge(m_done, hp * 8 + 8)

            def dve_part(dve, hp, nh, scored, exped, collect):
                for n in range(8):
                    dve.wait_ge(spread, hp * 8 + (n + 1))
                    dve.tensor_copy(mb[:, n // 2, 2 * (n % 2):2 * (n % 2) + 2, :], s_ps[:, n % RING, :, :]).then_inc(m_done, 1)
                dve.wait_ge(m_done, hp * 8 + 8)

                def clip(n):
                    lo = STEPS[n // 2][2]
                    dve.wait_ge(scored, hp * nh + (n + 1))
                    dve.wait_ge(exp_raw, hp * nh + (n + 1))
                    dve.tensor_scalar(a[:, n % 4, :, lo:], s_ps[:, n % RING, :, lo:], least, None, ALU.max).then_inc(freed, 1)
                    dve.wait_ge(freed, hp * nh + (n + 1 + RING))
                    dve.tensor_tensor(u[:, n % 4, :, lo:], a[:, n % 4, :, lo:], a[:, n % 4, :, lo:], ALU.mult).then_inc(clipped, 1)

                def plus(n):
                    lo = STEPS[n // 2][2]
                    dve.wait_ge(rooted, hp * nh + (n + 1))
                    dve.tensor_tensor(u[:, n % 4, :, lo:], a[:, n % 4, :, lo:], u[:, n % 4, :, lo:], ALU.add).then_inc(added, 1)

                def shift(n):
                    qc, _, lo = STEPS[n // 2]
                    half = n % 2
                    dve.wait_ge(logged, hp * nh + (n + 1))
                    dve.tensor_tensor(u[:, n % 4, :, lo:], u[:, n % 4, :, lo:], mb[:, qc, 2 * half:2 * half + 2, lo:],
                                      ALU.subtract).then_inc(shifted, 1)

                def hide(n):
                    qc, st, lo = STEPS[n // 2]
                    dve.wait_ge(exp_raw, hp * nh + (n + 5))
                    if st >= 4 * qc:
                        keep = masks["seen"].unsqueeze(1).to_broadcast([128, 2, 128])
                        dve.tensor_tensor(P[:, n % 4, :, lo:lo + 128], P[:, n % 4, :, lo:lo + 128], keep, ALU.mult).then_inc(exped, 1)
                    else:
                        dve.sem_inc(exped, 1)

                def pair(f, n):
                    if n < nh:
                        f(n)
                        f(n + 1)

                pair(clip, 0)
                pair(plus, 0)
                pair(clip, 2)
                for n in range(0, nh, 2):
                    pair(shift, n)
                    pair(plus, n + 2)
                    pair(hide, n)
                    if n + 2 == nh or STEPS[n // 2 + 1][0] > STEPS[n // 2][0]:
                        collect(STEPS[n // 2][0])
                    pair(clip, n + 4)

            def act_part(act, pairs, nh, scored, exped, summed):
                act.sem_inc(exped, RING)
                act.sem_inc(freed, RING)
                act.sem_inc(exp_raw, 4)
                act.preload_act_table_set("natural_log_exp_and_others")

                def root(hp, n):
                    lo = STEPS[n // 2][2]
                    at = u[:, n % 4, :, lo:]
                    act.wait_ge(clipped, hp * nh + (n + 1))
                    steps(act.activation(at, at, ACT.Ln, bias=C["minus_one"]))
                    act.activation(at, at, ACT.Exp, scale=0.5).then_inc(rooted, 1)

                def score(hp, n):
                    lo = STEPS[n // 2][2]
                    at = u[:, n % 4, :, lo:]
                    act.wait_ge(added, hp * nh + (n + 1))
                    steps(act.activation(at, at, ACT.Ln))
                    for v in range(2):
                        at_v = u[:, n % 4, v, lo:]
                        ins = act.activation(at_v, at_v, ACT.Ln, scale=roots[:, v:v + 1], bias=C["eps6"])
                    steps(ins)
                    act.activation(at, at, ACT.Exp, scale=-1.0).then_inc(logged, 1)

                def exps(hp, n):
                    lo = STEPS[n // 2][2]
                    act.wait_ge(shifted, hp * nh + (n + 1))
                    act.wait_ge(summed, hp * nh + (n + 1 - 4 + nh))
                    act.activation(P[:, n % 4, :, lo:], u[:, n % 4, :, lo:], ACT.Exp).then_inc(exp_raw, 1)

                steps = Steps(act, own_a)
                with steps.loop(pairs, 3 * nh + 1) as hp:
                    steps(act.activation(roots[:, :], W["hyp_root"][:, bass.ds(hp * 2, 2)], ACT.Copy))
                    for f in (root, score):
                        f(hp, 0)
                        f(hp, 1)
                    for n in range(0, nh, 2):
                        for f, at in ((root, n + 2), (exps, n), (score, n + 2)):
                            if at < nh:
                                f(hp, at)
                                f(hp, at + 1)

            return dict(load=load_m, pe=pe_part, dve=dve_part, act=act_part, freed=freed)

        causal_pass(nc, "hypb", loads, rows, N_HYP // 2, N_DOT, values, o_dram, z_dram, masks["big_kq"], ident_b, chain)



NH3, DH3, TOP3 = 8, 64, 3


def store_parts_by_chunk(nc, name, src, dram):
    with Scope(nc, name) as sc:
        parts, rest = sc.sb("parts", [128, 3, T], BF16), sc.sb("rest", [128, T])
        own, split, stored = sc.sem("dve_step"), sc.sem("split"), sc.sem("stored")
        with nc.Block() as block:
            @block.vector
            def _(dve):
                steps = Steps(dve, own)
                steps(dve.tensor_copy(parts[:, 0, :], src))
                steps(dve.tensor_tensor(rest[:, :], src, parts[:, 0, :], ALU.subtract))
                steps(dve.tensor_copy(parts[:, 1, :], rest[:, :]))
                dve.tensor_tensor(parts[:, 2, :], rest[:, :], parts[:, 1, :], ALU.subtract).then_inc(split, 1)

            @block.sync
            def _(sp):
                sp.wait_ge(split, 1)
                for q in range(3):
                    for c in range(16):
                        sp.dma_start(dram[q, :, :, c, :], parts[c * HD:(c + 1) * HD, q, :].rearrange("x (e t) -> x e t", t=128))\
                          .then_inc(stored, 16)
                sp.wait_ge(stored, 3 * 16 * 16)


def column_softmax_sums(nc, qd, kd, r_dram, inv_scale, minus_scale):
    NHD = B * 16
    with Scope(nc, "cs") as sc:
        rows = NP * HD
        q, k = sc.sb("q", [64 + rows, 2, S], BF16), sc.sb("k", [64 + rows, 2, S], BF16)
        E = sc.sb("E", [128, 4, 4, CH])
        mx, neg, z = sc.sb("mx", [128, 4, 2]), sc.sb("neg", [128, 4]), sc.sb("z", [128, 4, 2])
        rz, r_sb = sc.sb("rz", [128, 4, 1]), sc.sb("r_sb", [128, 2, CH])
        s_ps, r_ps = sc.ps("s_ps", [128, 7, CH]), sc.ps("r_ps", [128, CH])
        loaded, r_stored = [sc.sem("loaded0"), sc.sem("loaded1")], [sc.sem("r_stored0"), sc.sem("r_stored1")]
        s3_ready, s1_ready, neg_ready = sc.sem("s3_ready"), sc.sem("s1_ready"), sc.sem("neg_ready")
        exp1_done, exp3_done, rz_ready = sc.sem("exp1_done"), sc.sem("exp3_done"), sc.sem("rz_ready")
        r_done, r_copied, own, head_scored = sc.sem("r_done"), sc.sem("r_copied"), sc.sem("dve_step"), sc.sem("head_scored")
        sp_waits = sc.sem("sp_waits")
        N = 2 * ST
        n_dma = [0]

        def own_banks(n):
            return s_ps[:, 0:3, :] if n % 2 == 0 else s_ps[:, 4:7, :]

        with nc.Block() as block:
            @block.sync
            def _(sp):
                def get(it, p):
                    head = it * 2 + p
                    for copy in range(2):
                        for slot in range(NP):
                            at = slice(copy * 64 + slot * HD, copy * 64 + (slot + 1) * HD)
                            for dst, src, stack in ((q, qd, Q_STACK), (k, kd, K_STACK)):
                                sp.dma_start(dst[at, p, :], src[stack[slot], :, bass.ds(head, 1), :].rearrange("x e n -> x (e n)"))\
                                  .then_inc(loaded[p], 16)
                    n_dma[0] = 4 * NP

                def put(it, p):
                    wait(sp, r_copied, it * 2 + (p + 2), sp_waits)
                    sp.dma_start(r_dram[bass.ds(it * 2 + p, 1), :].rearrange("e (j n) -> (e j) n", j=4), r_sb[0:128:32, p, :]).then_inc(r_stored[p], 16)

                get(0, 0)
                get(0, 1)
                with sp.Fori(0, NHD // 2 - 1) as it:
                    for p in range(2):
                        wait(sp, head_scored, it * 2 + (p + 1), sp_waits)
                        get(it + 1, p)
                        put(it, p)
                for p in range(2):
                    put(NHD // 2 - 1, p)
                for p in range(2):
                    sp.wait_ge(r_stored[p], 16 * (NHD // 2) + 16)

            @block.tensor
            def _(pe):
                def score(it, n):
                    p, i = n // ST, n % ST
                    if i == 0:
                        pe.wait_ge(loaded[p], (it + 1) * (16 * n_dma[0]))

                    def product(a):
                        at = slice(64 * (a % 2), 64 * (a % 2) + rows)
                        out = own_banks(n)[:, a, :] if a < 3 else s_ps[:, 3, :]
                        return pe.matmul(out, k[at, p, i * 128:(i + 1) * 128], q[at, p, a * CH:(a + 1) * CH], start=True, stop=True)

                    pe.wait_ge(exp3_done, it * N + (n + 1))
                    for a in range(3):
                        mm = product(a)
                    mm.then_inc(s3_ready, 1)
                    pe.wait_ge(exp1_done, it * N + (n + 1))
                    product(3).then_inc(s1_ready, 1)

                def add_up(it, n):
                    p, i = n // ST, n % ST
                    pe.wait_ge(rz_ready, it * N + (n + 1))
                    if i == 0:
                        pe.wait_ge(r_copied, it * 2 + (p + 1))
                    w = rz[:, n % 4, :].to_broadcast([128, 32])
                    for a in range(4):
                        mm = pe.matmul(r_ps[32 * a:32 * a + 32, :], w, E[:, n % 4, a, :], start=(i == 0), stop=(i == ST - 1))
                    mm.then_inc(r_done, 1)

                with pe.Fori(0, NHD // 2) as it:
                    score(it, 0)
                    score(it, 1)
                    for n in range(2, N):
                        score(it, n)
                        add_up(it, n - 2)
                    add_up(it, N - 2)
                    add_up(it, N - 1)

            @block.scalar
            def _(act):
                with act.Fori(0, NHD // 2) as it:
                    for n in range(N):
                        act.wait_ge(neg_ready, it * N + (n + 1))
                        act.wait_ge(r_done, it * N + (n + 1))
                        act.activation(E[:, n % 4, 3, :], s_ps[:, 3, :], ACT.Exp, bias=neg[:, n % 4:n % 4 + 1], scale=inv_scale,
                                       accum_out=z[:, n % 4, 0:1]).then_inc(exp1_done, 1)
                        act.activation(E[:, n % 4, 0:3, :], own_banks(n), ACT.Exp, bias=neg[:, n % 4:n % 4 + 1], scale=inv_scale,
                                       accum_out=z[:, n % 4, 1:2]).then_inc(exp3_done, 1)

            @block.vector
            def _(dve):
                dve.sem_inc(exp3_done, 2)
                dve.sem_inc(exp1_done, 1)
                dve.sem_inc(r_done, 4)
                dve.sem_inc(r_copied, 1)
                for p in range(2):
                    dve.sem_inc(r_stored[p], 16)
                steps = Steps(dve, own)
                with steps.loop(NHD // 2, 2 * N) as it:
                    def maxima(n):
                        dve.wait_ge(s3_ready, it * N + (n + 1))
                        dve.tensor_reduce(mx[:, n % 4, 0:1], own_banks(n), AX.XY, ALU.max)
                        dve.wait_ge(s1_ready, it * N + (n + 1))
                        steps(dve.tensor_reduce(mx[:, n % 4, 1:2], s_ps[:, 3, :], AX.X, ALU.max))
                        dve.scalar_tensor_tensor(out=neg[:, n % 4:n % 4 + 1], in0=mx[:, n % 4, 0:1], scalar=mx[:, n % 4, 1:2],
                                                 in1=minus_scale, op0=ALU.max, op1=ALU.mult).then_inc(neg_ready, 1)

                    def weights(n):
                        dve.wait_ge(exp3_done, it * N + (n + 3))
                        steps(dve.tensor_tensor(z[:, n % 4, 0:1], z[:, n % 4, 0:1], z[:, n % 4, 1:2], ALU.add))
                        dve.wait_ge(r_done, it * N + (n + 1))
                        dve.reciprocal(rz[:, n % 4, :], z[:, n % 4, 0:1]).then_inc(rz_ready, 1)

                    def collect(p):
                        dve.wait_ge(r_done, it * N + ((p + 1) * ST + 4))
                        dve.wait_ge(r_stored[p], it * 16 + 16)
                        dve.tensor_copy(r_sb[:, p, :], r_ps[:, :]).then_inc(r_copied, 1)
                        dve.sem_inc(head_scored, 1)

                    maxima(0)
                    for n in range(1, N):
                        maxima(n)
                        weights(n - 1)
                        if n == ST + 1:
                            collect(0)
                    weights(N - 1)
                    collect(1)


def embed_attention(nc, x, xn, C, W, io):
    with Scope(nc, "l3a") as sc:
        qd = nc.dram_tensor("q3_parts", (3, HD, NT, 16, 128), BF16).ap()
        kd = nc.dram_tensor("k3_parts", (3, HD, NT, 16, 128), BF16).ap()
        r_dram = nc.dram_tensor("r3", (NT, S), F32).ap()
        a = sc.sb("a", [128, T])
        for n, dram in (("q", qd), ("k", kd)):
            linear(nc, f"l3{n}", [dict(terms=[(W["W" + n], xn)], dst=a, by="act", bias=W["b" + n])])
            store_parts_by_chunk(nc, f"l3parts{n}", a[:, :], dram)
        linear(nc, "l3v", [dict(terms=[(W["Wv"], xn)], dst=a, by="act", bias=W["bv"])])
        column_softmax_sums(nc, *(t.rearrange("q x e c t -> q x e (c t)") for t in (qd, kd)), r_dram, 1.0 / D, C["minus_inv_d"])
        r = sc.sb("r", [128, T])
        spread = r_dram.rearrange("e (c t) -> c e t", c=16)
        load(nc, "load_r", [(r[c * HD:(c + 1) * HD, :].rearrange("x (e t) -> x e t", t=128),
                             spread[c].unsqueeze(0).to_broadcast([HD, NT, 128])) for c in range(16)])
        small(nc, "vr", [("dve", lambda e: e.tensor_tensor(a[:, :], a[:, :], r[:, :], ALU.mult))])
        linear(nc, "l3o", [dict(terms=[(W["Wo"], a)], dst=x, by="dve", bias=W["bo"], add=x)])


def route_top3(nc, src, router, tri, s):
    with Scope(nc, "route3") as sc:
        sel, rank = sc.sb("sel", [128, NT, NH3]), sc.sb("rank", [128, NT, NH3])
        gt, eq = (sc.sb(n, [128, NT, NH3, NH3]) for n in ("gt", "eq"))
        ps = sc.ps("ps", [128, NT * NH3])
        own, logits_ready, scored = sc.sem("dve_step"), sc.sem("logits_ready"), sc.sem("scored")
        with nc.Block() as block:
            @block.tensor
            def _(pe):
                router_logits(pe, ps, src, router, NH3).then_inc(logits_ready, 1)

            @block.scalar
            def _(act):
                act.wait_ge(logits_ready, 1)
                act.activation(s.rearrange("p t e -> p (t e)"), ps[:, :], ACT.Sigmoid).then_inc(scored, 1)

            @block.vector
            def _(dve):
                steps = Steps(dve, own)
                dve.wait_ge(scored, 1)
                top_mask(dve, steps, s, sel[:, :, :], TOP3, NH3, tri, gt[:, :, :, :], eq[:, :, :, :], rank[:, :, :])
                steps(dve.tensor_tensor(s, s, sel[:, :, :], ALU.mult))


def start_output(nc, x, s, bo, ident, acc):
    with Scope(nc, "start") as sc:
        sT = sc.sb("sT", [NH3, 2, 4, 128])
        s_ps, a_ps = sc.ps("s_ps", [128, 2, CH]), sc.ps("a_ps", [128, 2, 4, 128])
        turned, turned_sb, added, copied = sc.sem("turned"), sc.sem("turned_sb"), sc.sem("added"), sc.sem("copied")
        with nc.Block() as block:
            @block.tensor
            def _(pe):
                for q in range(NT // 4):
                    if q >= 2:
                        pe.wait_ge(turned_sb, q - 1)
                    for t in range(4):
                        mm = pe.transpose(s_ps[0:NH3, q % 2, t * 128:(t + 1) * 128], s[:, 4 * q + t, :], ident)
                    mm.then_inc(turned, 1)
                    pe.wait_ge(turned_sb, q + 1)
                    if q >= 2:
                        pe.wait_ge(copied, q - 1)
                    for t in range(4):
                        tile = 4 * q + t
                        pe.matmul(a_ps[:, q % 2, t, :], x[:, tile * 128:(tile + 1) * 128], ident, start=True, stop=False)
                        mm = pe.matmul(a_ps[:, q % 2, t, :], sT[:, q % 2, t, :], bo, start=False, stop=True)
                    mm.then_inc(added, 1)

            @block.vector
            def _(dve):
                for q in range(NT // 4):
                    dve.wait_ge(turned, q + 1)
                    if q >= 2:
                        dve.wait_ge(added, q - 1)
                    dve.tensor_copy(sT[:, q % 2, :, :].rearrange("p t n -> p (t n)"), s_ps[0:NH3, q % 2, :]).then_inc(turned_sb, 1)
                    dve.wait_ge(added, q + 1)
                    dve.tensor_copy(acc[:, 4 * q:4 * q + 4, :], a_ps[:, q % 2, :, :]).then_inc(copied, 1)


def dense_attention(nc, qd, kd, vd, s, wo2, ident, minus_one, acc):
    NHD = B * NH3
    N = 2 * ST
    HS = S // 2
    with Scope(nc, "da") as sc:
        q, k = sc.sb("q", [128, 2, 3, S], BF16), sc.sb("k", [128, 2, 3, S], BF16)
        v = sc.sb("v", [128, 2, ST, DH3])
        E, ET = sc.sb("E", [128, 2, S]), sc.sb("ET", [128, 4, CH])
        mx, neg, z = sc.sb("mx", [128, 2, 2]), sc.sb("neg", [128, 2, 1]), sc.sb("z", [128, 2, 2])
        w, rz, o_sb = sc.sb("w", [128, 2, 1]), sc.sb("rz", [128, 2, 1]), sc.sb("o_sb", [128, 2, 128])
        s_ps, t_ps = sc.ps("s_ps", [128, S]), sc.ps("t_ps", [128, 2, CH])
        o_ps, y_ps = sc.ps("o_ps", [128, CH]), sc.ps("y_ps", [128, CH])
        loaded = [sc.sem("loaded0"), sc.sem("loaded1")]
        scored, neg_ready, exp_half = sc.sem("scored"), sc.sem("neg_ready"), sc.sem("exp_half")
        turned, et_copied = sc.sem("turned"), sc.sem("et_copied")
        o_copied, y_ready, y_added, own = sc.sem("o_copied"), sc.sem("y_ready"), sc.sem("y_added"), sc.sem("dve_step")
        sp_waits, weighed = sc.sem("sp_waits"), sc.sem("weighed")
        n_dma = [0]
        Q_PARTS, K_PARTS = ((0, 0), (0, 1), (1, 2)), ((0, 1), (2, 0), (1, 0))
        with nc.Block() as block:
            @block.sync
            def _(sp):
                def get(hd_b, hd_h, p):
                    n = 0
                    tok = bass.ds(hd_b * S, S)
                    for t in range(3):
                        for half in range(2):
                            at = slice(half * DH3, (half + 1) * DH3)
                            for dst, src, part in ((q, qd, Q_PARTS[t][half]), (k, kd, K_PARTS[t][half])):
                                sp.dma_start(dst[at, p, t, :], src[part, bass.ds(hd_h * DH3, DH3), tok]).then_inc(loaded[p], 16)
                                n += 1
                    sp.dma_start(v[:, p, :, :].rearrange("p t d -> p (t d)"),
                                 vd[bass.ds(hd_h, 1), :, bass.ds(hd_b * (ST * DH3), ST * DH3)].rearrange("h p n -> (h p) n")).then_inc(loaded[p], 16)
                    n_dma[0] = n + 1

                with sp.Fori(0, B) as b:
                    with sp.Fori(0, NH3 // 2) as hp:
                        for p in range(2):
                            wait(sp, y_ready, ((b * (NH3 // 2) + hp) * 2 + (p + 1)) * ST, sp_waits)
                            get(b, hp * 2 + p, p)

            @block.tensor
            def _(pe):
                pe.sem_inc(y_ready, 2 * ST)

                def heads(b, hp):
                    it = b * (NH3 // 2) + hp

                    def score(n):
                        p, i = n // ST, n % ST
                        if i == 0:
                            pe.wait_ge(loaded[p], (it + 1) * (16 * n_dma[0]))
                        for half in range(2):
                            pe.wait_ge(exp_half, (it * N + n) * 2 + (half + 1))
                            for t in range(3):
                                for c in range(2):
                                    at = slice((2 * half + c) * CH, (2 * half + c + 1) * CH)
                                    mm = pe.matmul(s_ps[:, at], q[:, p, t, i * 128:(i + 1) * 128], k[:, p, t, at],
                                                   start=(t == 0), stop=(t == 2))
                            mm.then_inc(scored, 1)

                    def turn(n, c):
                        pe.wait_ge(exp_half, (it * N + n) * 2 + (c // 2 + 3))
                        pe.wait_ge(et_copied, (it * N + n) * 4 + (c + 1))
                        for t in range(4):
                            mm = pe.transpose(t_ps[:, c % 2, t * 128:(t + 1) * 128],
                                              E[:, n % 2, (4 * c + t) * 128:(4 * c + t + 1) * 128], ident)
                        mm.then_inc(turned, 1)

                    def weigh(n, c):
                        pe.wait_ge(et_copied, (it * N + n) * 4 + (c + 3))
                        if c == 0:
                            pe.wait_ge(o_copied, it * N + (n + 1))
                        for t in range(4):
                            st = 4 * c + t
                            half = st % 2
                            mm = pe.matmul(o_ps[64 * half:64 * half + 64, 0:128], v[:, n // ST, st, :],
                                           ET[:, c, t * 128:(t + 1) * 128], start=(st < 2), stop=(st >= ST - 2))
                        mm.then_inc(weighed, 1)

                    def finish(n):
                        pe.wait_ge(o_copied, it * N + (n + 2))
                        pe.wait_ge(y_added, it * N + (n + 2))
                        pe.matmul(y_ps[:, 0:128], o_sb[:, n % 2, :], wo2[:, bass.ds(hp * 256 + (n // ST) * 128, 128)],
                                  start=True, stop=True).then_inc(y_ready, 1)

                    score(0)
                    for n in range(N):
                        if n + 1 < N:
                            score(n + 1)
                        if n:
                            finish(n - 1)
                        turn(n, 0)
                        turn(n, 1)
                        weigh(n, 0)
                        turn(n, 2)
                        weigh(n, 1)
                        turn(n, 3)
                        weigh(n, 2)
                        weigh(n, 3)
                    finish(N - 1)

                with pe.Fori(0, B) as b:
                    with pe.Fori(0, NH3 // 2) as hp:
                        heads(b, hp)

            @block.scalar
            def _(act):
                act.sem_inc(et_copied, 2)
                act.sem_inc(exp_half, 2)
                with act.Fori(0, NHD // 2) as it:
                    def exp(n, half):
                        if half == 0:
                            act.wait_ge(neg_ready, it * N + (n + 1))
                            act.wait_ge(turned, (it * N + n) * 4 + 4)
                        at = slice(half * HS, (half + 1) * HS)
                        act.activation(E[:, n % 2, at], s_ps[:, at], ACT.Exp, bias=neg[:, n % 2, :],
                                       accum_out=z[:, n % 2, half:half + 1]).then_inc(exp_half, 1)

                    def copy(n, c):
                        act.wait_ge(turned, (it * N + n) * 4 + (c + 9))
                        act.wait_ge(weighed, (it * N + n) * 4 + (c + 1))
                        act.activation(ET[:, c, :], t_ps[:, c % 2, :], ACT.Copy).then_inc(et_copied, 1)

                    exp(0, 0)
                    exp(0, 1)
                    for n in range(N):
                        copy(n, 0)
                        copy(n, 1)
                        if n + 1 < N:
                            exp(n + 1, 0)
                        copy(n, 2)
                        if n + 1 < N:
                            exp(n + 1, 1)
                        copy(n, 3)

            @block.vector
            def _(dve):
                dve.sem_inc(turned, 8)
                dve.sem_inc(weighed, 4)
                dve.sem_inc(o_copied, 1)
                dve.sem_inc(y_added, 2)

                def heads(b, hp, steps, it):
                    def maxima(n):
                        for half in range(2):
                            dve.wait_ge(scored, (it * N + n) * 2 + (half + 1))
                            ins = dve.tensor_reduce(mx[:, n % 2, half:half + 1], s_ps[:, half * HS:(half + 1) * HS], AX.X, ALU.max)
                        steps(ins)
                        dve.scalar_tensor_tensor(out=neg[:, n % 2, :], in0=mx[:, n % 2, 0:1], scalar=mx[:, n % 2, 1:2],
                                                 in1=minus_one, op0=ALU.max, op1=ALU.mult).then_inc(neg_ready, 1)

                    def weight(n):
                        p, i = n // ST, n % ST
                        wait(dve, exp_half, (it * N + n) * 2 + 4)
                        steps(dve.tensor_tensor(z[:, n % 2, 0:1], z[:, n % 2, 0:1], z[:, n % 2, 1:2], ALU.add))
                        steps(dve.reciprocal(rz[:, n % 2, :], z[:, n % 2, 0:1]))
                        dve.wait_ge(y_added, it * N + (n + 1))
                        steps(dve.tensor_tensor(w[:, n % 2, :], rz[:, n % 2, :],
                                                s[:, bass.ds((b * ST + i) * NH3 + hp * 2 + p, 1)], ALU.mult))

                    def collect(n):
                        dve.wait_ge(weighed, (it * N + n) * 4 + 8)
                        dve.wait_ge(y_ready, it * N + (n + 2 * ST - 1))
                        dve.tensor_copy(o_sb[:, n % 2, :], o_ps[:, 0:128]).then_inc(o_copied, 1)

                    def add(n):
                        dve.wait_ge(y_ready, it * N + (n + 2 * ST + 1))
                        tile = acc[:, bass.ds((b * ST + n % ST) * D, D)]
                        dve.scalar_tensor_tensor(out=tile, in0=y_ps[:, 0:128], scalar=w[:, n % 2, :], in1=tile,
                                                 op0=ALU.mult, op1=ALU.add).then_inc(y_added, 1)

                    maxima(0)
                    for n in range(N):
                        if n + 1 < N:
                            maxima(n + 1)
                        weight(n)
                        if n:
                            add(n - 1)
                        collect(n)
                    add(N - 1)

                steps = Steps(dve, own)
                with dve.Fori(0, B) as b:
                    with dve.Fori(0, NH3 // 2) as hp:
                        it = b * (NH3 // 2) + hp
                        steps.base, steps.k = it * (4 * N), 0
                        heads(b, hp, steps, it)
                        assert steps.k == 4 * N


def project_parts(nc, xn, jobs):
    with Scope(nc, "pp") as sc:
        parts = sc.sb("parts", [128, 2, 3, T], BF16)
        rest = sc.sb("rest", [128, 4, CH])
        ps = sc.ps("ps", [128, 4, CH])
        made, high, rested, mid, low = (sc.sem(n) for n in ("made", "high", "rested", "mid", "low"))
        stored = [sc.sem("stored0"), sc.sem("stored1")]
        steps = [(j, c) for j in range(len(jobs)) for c in range(NC)]
        with nc.Block() as block:
            @block.tensor
            def _(pe):
                for n, (j, c) in enumerate(steps):
                    if n >= 4:
                        pe.wait_ge(rested, n - 3)
                    pe.matmul(ps[:, n % 4, :], jobs[j][0], cols(xn, c), start=True, stop=True).then_inc(made, 1)

            @block.scalar
            def _(act):
                def middle(n):
                    j, c = steps[n]
                    act.wait_ge(rested, n + 1)
                    act.activation(parts[:, j % 2, 1, c * CH:(c + 1) * CH], rest[:, n % 4, :], ACT.Copy).then_inc(mid, 1)

                for n, (j, c) in enumerate(steps):
                    if c == 0 and j >= 2:
                        act.wait_ge(stored[j % 2], 48 * (j // 2))
                    act.wait_ge(made, n + 1)
                    act.activation(parts[:, j % 2, 0, c * CH:(c + 1) * CH], ps[:, n % 4, :], ACT.Copy, scale=jobs[j][1]).then_inc(high, 1)
                    if n:
                        middle(n - 1)
                middle(len(steps) - 1)

            @block.vector
            def _(dve):
                def last(n):
                    j, c = steps[n]
                    dve.wait_ge(mid, n + 1)
                    at = slice(c * CH, (c + 1) * CH)
                    dve.tensor_tensor(parts[:, j % 2, 2, at], rest[:, n % 4, :], parts[:, j % 2, 1, at], ALU.subtract).then_inc(low, 1)

                for n, (j, c) in enumerate(steps):
                    dve.wait_ge(high, n + 1)
                    if n >= 4:
                        dve.wait_ge(low, n - 3)
                    dve.scalar_tensor_tensor(out=rest[:, n % 4, :], in0=ps[:, n % 4, :], scalar=jobs[j][1],
                                             in1=parts[:, j % 2, 0, c * CH:(c + 1) * CH], op0=ALU.mult, op1=ALU.subtract)\
                       .then_inc(rested, 1)
                    if n >= 2:
                        last(n - 2)
                last(len(steps) - 2)
                last(len(steps) - 1)

            @block.sync
            def _(sp):
                for j, (_, _, dram) in enumerate(jobs):
                    sp.wait_ge(low, NC * (j + 1))
                    for q in range(3):
                        sp.dma_start(dram[q], parts[:, j % 2, q, :]).then_inc(stored[j % 2], 16)
                for p in range(2):
                    sp.wait_ge(stored[p], 48 * (len(jobs) // 2))


def project_values(nc, xn, w, vd):
    G = 8
    with Scope(nc, "pv") as sc:
        V = sc.sb("V", [128, 2, NH3, G, DH3])
        ps = sc.ps("ps", [128, 4, CH])
        made, copied, stored = sc.sem("made"), sc.sem("copied"), [sc.sem("stored0"), sc.sem("stored1")]
        with nc.Block() as block:
            @block.tensor
            def _(pe):
                for t in range(NT):
                    if t >= 4:
                        pe.wait_ge(copied, t - 3)
                    pe.matmul(ps[:, t % 4, :], xn[:, t * 128:(t + 1) * 128], w, start=True, stop=True).then_inc(made, 1)

            @block.scalar
            def _(act):
                for t in range(NT):
                    g = t // G
                    if t % G == 0 and g >= 2:
                        act.wait_ge(stored[g % 2], 16 * NH3 * (g // 2))
                    act.wait_ge(made, t + 1)
                    act.activation(V[:, g % 2, :, t % G, :], ps[:, t % 4, :].rearrange("p (h d) -> p h d", h=NH3), ACT.Copy)\
                       .then_inc(copied, 1)

            @block.sync
            def _(sp):
                for g in range(NT // G):
                    sp.wait_ge(copied, G * (g + 1))
                    for h in range(NH3):
                        sp.dma_start(vd[h, :, g * G:(g + 1) * G, :], V[:, g % 2, h, :, :]).then_inc(stored[g % 2], 16)
                for p in range(2):
                    sp.wait_ge(stored[p], 16 * NH3 * (NT // G // 2))


def routed_attention(nc, x, xn, C, W, acc):
    with Scope(nc, "l3f") as sc:
        qd = nc.dram_tensor("qf_parts", (3, NH3 * DH3, T), BF16).ap()
        kd = nc.dram_tensor("kf_parts", (3, NH3 * DH3, T), BF16).ap()
        vd = nc.dram_tensor("vf", (NH3, 128, NT, DH3), F32).ap()
        s = sc.sb("s", [128, NT, NH3])
        route_top3(nc, xn, W["Ws"], C["tri8"], s[:, :, :])
        project_parts(nc, xn, [(W["FWq"][:, j * 128:(j + 1) * 128], DH3 ** -0.5, qd[:, j * 128:(j + 1) * 128, :]) for j in range(4)] +
                      [(W["FWk"][:, j * 128:(j + 1) * 128], 1.0, kd[:, j * 128:(j + 1) * 128, :]) for j in range(4)])
        project_values(nc, xn, W["FWv"], vd)
        start_output(nc, x, s, W["bo3"], C["ident"], acc)
        dense_attention(nc, qd, kd, vd.rearrange("h p t d -> h p (t d)"), s[:, :, :].rearrange("p t e -> p (t e)"), W["wo2"],
                        C["ident"], C["minus_one"], acc[:, :, :].rearrange("p t d -> p (t d)"))


def store(nc, pairs, name="store"):
    with Scope(nc, name) as sc:
        stored = sc.sem("stored")
        with nc.Block() as block:
            @block.sync
            def _(sp):
                for dst, src in pairs:
                    sp.dma_start(dst, src).then_inc(stored, 16)
                sp.wait_ge(stored, 16 * len(pairs))


def add_in_place(nc, name, dst, other):
    with Scope(nc, name) as sc:
        added = sc.sem("added")
        with nc.Block() as block:
            @block.vector
            def _(dve):
                dve.tensor_tensor(dst[:, :], dst[:, :], other, ALU.add).then_inc(added, 1)


def mamba(nc, x, xn, C, io):
    pm, pf = PACKS["m"], PACKS["f"]
    with Scope(nc, "mamba") as sc:
        pad = K_CONV - 1
        xs, zs = sc.sb("xs", [128, 2, T]), sc.sb("zs", [128, 2, T])
        dts = sc.sb("dts", [128, 2 * (T + B * pad)])
        xpre = dts[:, :].rearrange("p (h n) -> p h n", h=2)
        dt = dts[:, 0:2 * T].rearrange("p (h n) -> p h n", h=2)
        wt, bc = sc.sb("wt", [128, pm.n]), sc.sb("bc", [96, T], BF16)
        W = {k: pm.view(wt, k) for k in pm.at}
        load(nc, "load_m", [(wt[:, :], io["pack_m"])])
        with Scope(nc, "mamba_in") as si:
            hm = si.sb("hm", [128, T])
            norm(nc, "rms_in", xn, hm, C["ones"], C["eps6"], center=False, gain=W["in_ln"])
            small(nc, "pads", [("dve", lambda e, h=h, b=b: e.memset(xpre[:, h, b * (S + pad):b * (S + pad) + pad], 0.0))
                               for h in range(2) for b in range(B)] + [
                ("act", lambda e: e.activation(W["A_log"], W["A_log"], ACT.Exp)),
                ("dve", lambda e: e.tensor_scalar(W["A_log"], W["A_log"], -1.0, None, ALU.mult))])
            linear(nc, "in_proj", [
                dict(terms=[(W["in_proj"][:, h * 128:(h + 1) * 128], hm)], dst=xpre[:, h, :], pad=pad, by="dve") for h in range(2)] + [
                dict(terms=[(W["in_proj"][:, (2 + h) * 128:(3 + h) * 128], hm)], dst=zs[:, h, :], by="act", func=ACT.Silu)
                for h in range(2)])
            conv_silu(nc, xpre, xs, W["conv_w"], W["conv_b"])
            linear(nc, "x_proj_dt", [
                dict(terms=[(W["xp_dt"][:, h * 64:(h + 1) * 64], xs[:, h, :]) for h in range(2)], dst=hm[0:64, :], by="dve")])
            norm(nc, "rms_dt", hm[0:64, :], hm[0:64, :], C["ones64"], C["eps6"], center=False, gain=W["dt_ln"], rows=64)
            linear(nc, "dt_proj", [
                dict(terms=[(W["dt_proj"][:, h * 128:(h + 1) * 128], hm[0:64, :])], dst=dt[:, h, :], by="act",
                     bias=W["dt_b"][:, h:h + 1]) for h in range(2)])
            linear(nc, "x_proj_bc", [
                dict(terms=[(W["xp_bc"][:, h * 96:(h + 1) * 96], xs[:, h, :]) for h in range(2)], dst=hm[0:96, :], by="dve")])
            norm(nc, "rms_bc", hm[0:96, :], hm[0:96, :], C["bcmean"], C["eps6"], center=False, gain=W["bc_ln"], rows=96)
            split3(nc, "split_bc", hm[0:96, :], bc, 96, 32)
            softplus(nc, dt, hm)
        with Scope(nc, "mamba_scan") as ss:
            bc_sel = ss.sb("bc_sel", [96, 2 * D_STATE * 128], BF16)
            load(nc, "load_sel", [(bc_sel[:, :], io["bc_sel"])])
            selective_scan(nc, dt, xs, zs, bc, bc_sel, W["A_log"], W["D_skip"], C["ident"])
        with Scope(nc, "mamba_out") as so:
            ft = so.sb("ft", [128, pf.n])
            F = {k: pf.view(ft, k) for k in pf.at}
            load(nc, "load_f", [(ft[:, :], io["pack_f"])])
            hid, hn = dt[:, 0, :], dt[:, 1, :]
            linear(nc, "out_proj", [
                dict(terms=[(W["out_proj"][:, h * 128:(h + 1) * 128], xs[:, h, :]) for h in range(2)], dst=hid, by="dve", add=xn)])
            norm(nc, "rms_ff", hid, hn, C["ones"], C["eps6"], center=False, gain=W["ff_ln"])
            add_in_place(nc, "add_hid", x, hid)
            expert_blocks(nc, "ff", hn, [
                dict(gate=F["gate"][:, j * 128:(j + 1) * 128], up=F["up"][:, j * 128:(j + 1) * 128], func=ACT.Silu,
                     down=F["down"][:, j * 128:(j + 1) * 128]) for j in range(4)], None, x, x)



def layouts(i):
    def blocks(w, rows=128):
        k = w.shape[0] // rows
        return w.reshape(k, rows, w.shape[1]).transpose(1, 0, 2).reshape(rows, -1)

    def col(v):
        return v.reshape(-1, 128).T

    eye = np.eye(128, dtype=np.float32)
    bcmean = np.kron(np.eye(6), np.full((16, 16), 1 / 16)).astype(np.float32)
    c = dict(ones=np.full((128, 128), 1 / 128), ones64=np.full((64, 128), 1 / 64), bcmean=bcmean, ident=eye,
             eps5=np.full((128, 1), 1e-5), eps6=np.full((128, 1), 1e-6), one=np.ones((128, 1)), minus_one=-np.ones((128, 1)), minus_inv_d=np.full((128, 1), -1 / D),
             tri8=np.tile(np.tril(np.ones((8, 8)), -1).reshape(1, -1), (128, 1)),
             tri4=np.tile(np.tril(np.ones((4, 4)), -1).reshape(1, -1), (128, 1)))
    xp = i["L0_attn_x_proj_w"]
    m = dict(in_proj=i["L0_attn_in_proj_w"], conv_w=blocks(i["L0_attn_conv_w"]), conv_b=col(i["L0_attn_conv_b"]),
             xp_dt=blocks(xp[:, :DT_RANK]), xp_bc=blocks(np.concatenate([xp[:, DT_RANK:]] * 3, axis=1)),
             dt_proj=i["L0_attn_dt_proj_w"], dt_b=col(i["L0_attn_dt_proj_b"]), dt_ln=i["L0_attn_dt_ln_w"],
             bc_ln=np.concatenate([i["L0_attn_b_ln_w"], i["L0_attn_c_ln_w"]] * 3), A_log=blocks(i["L0_attn_A_log"]),
             D_skip=col(i["L0_attn_D_skip"]), out_proj=blocks(i["L0_attn_out_proj_w"]),
             in_ln=i["L0_attn_input_ln_w"], ff_ln=i["L0_attn_pre_moe_ln_w"])
    f = dict(gate=i["L0_attn_gate_w"], up=i["L0_attn_up_w"], down=blocks(i["L0_attn_down_w"]))
    e = dict(router=i["L0_ffn_gate_w"].T, gate=i["L0_ffn_expert_gate"].reshape(-1, D).T,
             up=i["L0_ffn_expert_up"].reshape(-1, D).T, down=blocks(i["L0_ffn_expert_down"].transpose(0, 2, 1).reshape(-1, D)),
             sgate=i["L0_ffn_shared_gate_w"].T, sup=i["L0_ffn_shared_up_w"].T, sdown=i["L0_ffn_shared_down_w"].T)
    a = lambda n: i["L1_attn_" + n]
    b = lambda n: i["L1_ffn_" + n]
    l1 = dict(Wk=a("Wk").T, Wka=a("Wka").T, Wv=a("Wv").T, ce_syn=b("ce_syn_w"), ce_synT=b("ce_syn_w").T, ce_wv=b("ce_wv"),
              ce_wo=b("ce_wo"), me_eqT=b("me_eq_w").T, me_wv=b("me_wv"), me_wo=b("me_wo"), gen=b("ce_gen_w"),
              ones_row=np.ones((128, 128)), bk=a("bk"), bka=a("bka"), bv=a("bv"), gamma=a("gamma"), beta=a("beta"),
              me_eqb=b("me_eq_b"), me_bv=b("me_bv"), me_bo=b("me_bo"), me_c2b=b("me_c2b"), ce_synb=b("ce_syn_b"),
              ce_bv=b("ce_bv"), ce_bo=b("ce_bo"), n1g=b("ce_n1g"), n1b=b("ce_n1b"), f2b=b("ce_f2b"), n2g=b("ce_n2g"),
              n2b=b("ce_n2b"), gen_b=b("ce_gen_b"), ml_b2=b("ml_b2"), router=b("router_w"), router_b=b("router_b"),
              balancer=b("load_balancer"), me_c1=b("me_c1w"), me_c1b=col(b("me_c1b")), me_c2=blocks(b("me_c2w")),
              f1=b("ce_f1w"), f1b=col(b("ce_f1b")), f2=blocks(b("ce_f2w")), sw1=b("sw_w1"), sw3=b("sw_w3"),
              sw2=blocks(b("sw_w2")), ml1=b("ml_w1"), ml_b1=col(b("ml_b1")), ml2=blocks(b("ml_w2")))
    qkv = i["L2_attn_qkv_w"]
    swap = (np.arange(128) // HD) * HD + (np.arange(128) + HD // 2) % HD
    head = np.arange(128) // HD
    dot, hyp = head < N_DOT, (head >= N_DOT) & (head < N_DOT + N_HYP)
    cosine = head >= N_DOT + N_HYP
    curv = i["L2_attn_curvature"].reshape(-1)
    c_rows = np.ones(128, np.float32)
    c_rows[N_DOT * HD:(N_DOT + N_HYP) * HD] = np.repeat(curv, HD)
    one_of = lambda mask, v: np.where(mask, np.float32(v), np.float32(0))
    key, query = np.arange(128)[:, None], np.arange(128)[None, :]
    l2 = dict(Wq=qkv[0:128].T, Wqs=qkv[0:128].T[:, swap], Wk=qkv[128:256].T, Wks=qkv[128:256].T[:, swap], Wv=qkv[256:].T,
              Wo=i["L2_attn_proj_w"].T, bin=i["L2_ffn_weight"].T, blocks8=np.kron(np.eye(16), np.ones((8, 8))),
              seen=(key <= query), c=c_rows, inv_c=np.zeros(128), hyp=one_of(hyp, 1), q_base=one_of(dot, HD ** -0.5),
              q_cos=one_of(cosine, HD ** 0.5), k_base=one_of(~cosine, 1), k_cos=one_of(cosine, 1),
              root_inv_c=np.zeros(128), proj_b=i["L2_attn_proj_b"], hyp_c=np.broadcast_to(curv, (128, N_HYP)),
              hyp_root=np.zeros((128, N_HYP)))
    a3 = {n: i["L3_attn_" + n] for n in ("Wq", "Wk", "Wv", "Wo", "bq", "bk", "bv", "bo")}
    wo = i["L3_ffn_Wo"]
    l3 = dict(a3, FWq=i["L3_ffn_Wq"], FWk=i["L3_ffn_Wkv"][:, :512], FWv=i["L3_ffn_Wkv"][:, 512:], Ws=i["L3_ffn_Ws"],
              wo2=np.concatenate([wo, wo], axis=1).transpose(1, 0, 2), bo3=i["L3_ffn_bo"])
    parts = dict(c=c, m=m, f=f, e=e, l1=l1, l2=l2, l3=l3)
    out_sel1 = selector(12, 4, [(q * 4 + v, v, slice(0, 128)) for v in range(4) for q in range(3)])
    out = {"x": i["L0_attn_hidden_states"].reshape(T, D).T}
    for name, p in parts.items():
        out[f"pack_{name}"] = PACKS[name].fill(p)
    out["bc_sel"] = selector(96, 32, [(p, n, slice(0, 128)) for n in range(32) for p in (n, 32 + n, 64 + n)])
    out["moe_sel"] = selector(96, 16, [(q * 32 + 2 * j + v, j, slice(64 * v, 64 * v + 64))
                                       for j in range(16) for v in range(2) for q in range(3)])
    out["sel1"] = out_sel1
    inv_freq = 1.0 / 10000.0 ** (np.arange(0, HD, 2, dtype=np.float32) / np.float32(HD))
    angle = np.outer(np.arange(S, dtype=np.float32), inv_freq.astype(np.float32)).astype(np.float32).T
    cos, sin = np.cos(angle).astype(np.float32), np.sin(angle).astype(np.float32)
    out["rot_cos"] = np.tile(np.concatenate([cos, cos]), (HEADS, 1))
    out["rot_sin"] = np.tile(np.concatenate([sin, -sin]), (HEADS, 1))
    b16 = mybir.dt.np(BF16)
    out["ones_b"] = np.ones((3, S), b16)
    hidden = (key > query)
    out["masks"] = np.concatenate([np.where(hidden.T, -1e30, 0), np.where(hidden, -1e30, 0), np.where(hidden.T, BIG, 0),
                                   np.where(hidden, BIG, 0)], axis=1).astype(b16)
    out["ident_b"] = selector(128, 1, [(p, 0, p) for p in range(128)])
    return out


def selector(rows, blocks, ones):
    s = np.zeros((rows, blocks, 128), mybir.dt.np(BF16))
    for row, block, columns in ones:
        s[row, block, columns] = 1
    return s.reshape(rows, blocks * 128)


def kernel(**inputs):
    import concourse.bacc as bacc
    from concourse.bass_utils import run_bass_kernel_spmd

    nc = bacc.Bacc("TRN2", target_bir_lowering=False, num_devices=1)
    arrays, io = {}, {}
    for name, a in layouts({k: np.asarray(v) for k, v in inputs.items()}).items():
        arrays[f"in_{name}"] = np.ascontiguousarray(a)
        io[name] = nc.dram_tensor(f"in_{name}", a.shape, mybir.dt.from_np(a.dtype), kind="ExternalInput").ap()
    io["out"] = nc.dram_tensor("out_0", (T, D), F32, kind="ExternalOutput").ap()
    build(nc, io)
    r = run_bass_kernel_spmd(nc, [arrays], core_ids=[0])
    return r.results[0]["out_0"].reshape(B, S, D)
```
